# Optimizing a Trainium2 kernel written in Bass

```python
import numpy as np
import jax
import jax.numpy as jnp

def _softmax(x, axis=-1):
    return jax.nn.softmax(x, axis=axis)

def _gelu(x):
    return jax.nn.gelu(x, approximate=True)

def _silu(x):
    return jax.nn.silu(x)

def _sigmoid(x):
    return jax.nn.sigmoid(x)

def _layernorm(x, axis=-1, eps=1e-05):
    m = jnp.mean(x, axis=axis, keepdims=True)
    v = jnp.var(x, axis=axis, keepdims=True)
    return (x - m) / jnp.sqrt(v + eps)

def _scatter_add(tgt, idx, src, axis=0):
    return tgt.at[idx].add(src)

def _segment_sum(src, seg, n):
    return jax.ops.segment_sum(src, seg, n)
kernel_name = 'mk_gnn_resnorm_d1_gnn_r64_a62aba'

def setup_inputs(seed: int=0):
    np.random.seed(seed)
    _w = jnp.asarray

    def _rec_inputs():
        import jax
        import jax.numpy as jnp
        _gk = jax.random.key(seed)
        x = -0.0003713 + 1 * jax.random.normal(jax.random.fold_in(_gk, 1), (100000, 128), jnp.float32)
        src = jax.random.randint(jax.random.fold_in(_gk, 2), (50000,), 0, 100000, jnp.int32)
        dst = jnp.minimum((100000 * jax.random.uniform(jax.random.fold_in(_gk, 3), (50000,)) ** 2.0).astype(jnp.int32), 99999)
        _o = jnp.argsort(dst, stable=True)
        src = src[_o]
        dst = dst[_o]
        edge_attr_64 = 0.000155561 + 1.00019 * jax.random.normal(jax.random.fold_in(_gk, 11), (50000, 64), jnp.float32)
        return (x, src, dst, edge_attr_64)
    x, src, dst, edge_attr_64 = _rec_inputs()

    def _L0_gnn_setup():
        import jax, jax.numpy as jnp
        import numpy as np
        N, E, D, ED = (100000, 9375, 128, 64)
        RMS_EPS = 1.1920929e-07
        DEG_POWER = 0.5
        key = jax.random.key(seed)
        ks = jax.random.split(key, 12)
        s = 0.05
        return {'x': jax.random.normal(ks[0], (N, D), jnp.float32), 'edge_index': jax.random.randint(ks[1], (2, E), 0, N, jnp.int32), 'edge_attr': jax.random.normal(ks[2], (E, ED), jnp.float32), 'W1n': jax.random.normal(ks[3], (D, D), jnp.float32) * s, 'b1n': jnp.zeros((D,), jnp.float32), 'W2n': jax.random.normal(ks[4], (D, D), jnp.float32) * s, 'b2n': jnp.zeros((D,), jnp.float32), 'W1e': jax.random.normal(ks[5], (ED, D), jnp.float32) * s, 'b1e': jnp.zeros((D,), jnp.float32), 'W2e': jax.random.normal(ks[6], (D, D), jnp.float32) * s, 'b2e': jnp.zeros((D,), jnp.float32), 'gin_eps': jnp.float32(0.0), 'rms_w': jnp.ones((D,), jnp.float32)}
    _L0_gnn_all = _L0_gnn_setup()
    _L0_gnn_in = {k: v for k, v in _L0_gnn_all.items() if k in ('W1n', 'b1n', 'W2n', 'b2n', 'W1e', 'b1e', 'W2e', 'b2e', 'gin_eps', 'rms_w')}
    del _L0_gnn_all
    return {'x': x, 'src': src, 'dst': dst, 'edge_attr_64': edge_attr_64, 'L0_gnn_W1n': _L0_gnn_in['W1n'], 'L0_gnn_b1n': _L0_gnn_in['b1n'], 'L0_gnn_W2n': _L0_gnn_in['W2n'], 'L0_gnn_b2n': _L0_gnn_in['b2n'], 'L0_gnn_W1e': _L0_gnn_in['W1e'], 'L0_gnn_b1e': _L0_gnn_in['b1e'], 'L0_gnn_W2e': _L0_gnn_in['W2e'], 'L0_gnn_b2e': _L0_gnn_in['b2e'], 'L0_gnn_gin_eps': _L0_gnn_in['gin_eps'], 'L0_gnn_rms_w': _L0_gnn_in['rms_w']}

def reference(x, src, dst, edge_attr_64, L0_gnn_W1n, L0_gnn_b1n, L0_gnn_W2n, L0_gnn_b2n, L0_gnn_W1e, L0_gnn_b1e, L0_gnn_W2e, L0_gnn_b2e, L0_gnn_gin_eps, L0_gnn_rms_w):
    import jax
    import jax.numpy as jnp

    def _L0_gnn_ref(x, edge_index, edge_attr, W1n, b1n, W2n, b2n, W1e, b1e, W2e, b2e, gin_eps, rms_w):
        import jax, jax.numpy as jnp
        import numpy as np
        N, E, D, ED = (100000, 9375, 128, 64)
        RMS_EPS = 1.1920929e-07
        DEG_POWER = 0.5
        src, dst = (edge_index[0], edge_index[1])
        n = x.shape[0]
        deg = jnp.maximum(jnp.zeros((n,), x.dtype).at[dst].add(1.0), 1.0)
        edge_weight = (deg[src] * deg[dst]) ** (-DEG_POWER)
        edge_msg = jax.nn.relu(edge_attr @ W1e + b1e) @ W2e + b2e
        messages = (x[src] + edge_msg) * edge_weight[:, None]
        agg = jax.ops.segment_sum(messages, dst, num_segments=n)
        combined = (1.0 + gin_eps) * x + agg
        h = jax.nn.relu(combined @ W1n + b1n) @ W2n + b2n
        out = h + x
        out = out * jax.lax.rsqrt(jnp.mean(out * out, axis=-1, keepdims=True) + RMS_EPS) * rms_w
        return out
    edge_index = jnp.stack([src, dst])
    x = _layernorm(x + _L0_gnn_ref(x, edge_index, edge_attr_64, L0_gnn_W1n, L0_gnn_b1n, L0_gnn_W2n, L0_gnn_b2n, L0_gnn_W1e, L0_gnn_b1e, L0_gnn_W2e, L0_gnn_b2e, L0_gnn_gin_eps, L0_gnn_rms_w), axis=-1)
    return x

_drawn_inputs = setup_inputs


def setup_inputs(seed=0):
    import zlib

    import numpy as np

    out = dict(_drawn_inputs(seed))
    spreads = {'L0_gnn_b1n': (0.0, 0.413),
     'L0_gnn_b2n': (0.0, 0.1),
     'L0_gnn_b1e': (0.0, 2.0),
     'L0_gnn_b2e': (0.0, 2.0),
     'L0_gnn_rms_w': (1.0, 0.2)}
    factors = {'edge_attr_64': 6.833, 'L0_gnn_W1e': 6.826, 'L0_gnn_W2e': 5.415}
    for name, (base, spread) in spreads.items():
        noise = np.random.default_rng([zlib.crc32(name.encode()), seed]).standard_normal(out[name].shape)
        drawn = base * np.exp(spread * noise) if base else spread * noise
        out[name] = jnp.asarray(drawn.astype(out[name].dtype))
    for name, factor in factors.items():
        out[name] = (out[name] * factor).astype(out[name].dtype)
    return out
```

```python
import concourse.bass as bass
from concourse import mybir
from contextlib import ExitStack


class Count:

    def __init__(self, i, per, base):
        self.i, self.per, self.base = i, per, base

    def __add__(self, k):
        return Count(self.i, self.per, self.base + k)

    def __sub__(self, k):
        return Count(self.i, self.per, self.base - k)

    def __mul__(self, k):
        return Count(self.i, self.per * k, self.base * k)

    def __floordiv__(self, k):
        assert self.per % k == 0
        return Count(self.i, self.per // k, self.base // k)

    def value(self):
        return self.i * self.per + self.base if self.base >= 0 else self.i * self.per - -self.base


def build(nc, x, src, dst, edge_attr, W1n, b1n, W2n, b2n, W1e, b1e, W2e, b2e, gin_eps, rms_w, out):
    f32 = mybir.dt.float32
    bf16 = mybir.dt.bfloat16
    f16 = mybir.dt.float16
    i32 = mybir.dt.int32
    ALU = mybir.AluOpType
    ACT = mybir.ActivationFunctionType

    P = 128
    N, D = x.shape
    E, ED = edge_attr.shape
    RMS_EPS = 1.1920929e-07
    LN_EPS = 1e-05

    TB = 4
    W = TB * P
    TILES = -(-E // P)
    BATCHES = -(-TILES // TB)
    BATCHES += BATCHES % 2
    FULL = E // P
    REST = E - FULL * P
    CH = TB
    assert BATCHES * TB <= CH * P and FULL // P == CH - 1
    NO_NODE = 2 * N
    SKIP = 1000000.0

    HIGH = -(-N // P)
    HIGH += HIGH % 2
    HCH = -(-HIGH // P)

    NPP = N // P
    NREM = N - NPP * P
    BN = 8
    BLOCKS = -(-(NPP + 1) // BN)
    LASTC = NPP - (BLOCKS - 1) * BN
    assert 0 < LASTC < BN
    STEPS = 2 * BLOCKS
    XR = 4

    agg_d = nc.dram_tensor("agg_scratch", (N, D), f32)
    tab_d = nc.dram_tensor("rsqrt_degree_scratch", (HCH * P * P, 1), f32)
    seg_d = nc.dram_tensor("segment_number_scratch", (CH * P * P,), bf16)
    agg_rows = agg_d[:, :]
    tab_rows = tab_d[:, :]

    with ExitStack() as ctx:
        def sb(name, shape, dt=f32):
            return ctx.enter_context(nc.sbuf_tensor(name, shape, dt))

        def sem(name):
            return ctx.enter_context(nc.semaphore(name))

        def sems(name, n):
            return [sem(f"{name}{i}") for i in range(n)]

        ident = sb("ident", [P, P])
        iota_i = sb("iota_i", [P, HIGH], i32)
        iota_h = sb("iota_h", [P, HIGH], f16)
        gidx_i = sb("gidx_i", [P, CH, P], i32)
        gidx = sb("gidx", [P, CH, P])
        ones = sb("ones", [P, P])
        ones_b = sb("ones_b", [P, P], bf16)
        zeros = sb("zeros", [P, 4096])
        w1e = sb("w1e", [ED, D])
        w2e = sb("w2e", [D, D])
        w1n = sb("w1n", [D, D])
        w2n = sb("w2n", [D, D])
        b1e_c = sb("b1e_c", [D, 1])
        b1n_c = sb("b1n_c", [D, 1])
        rms_b = sb("rms_b", [P, D])
        eps1 = sb("eps1", [P, 1])
        bias_f = sb("bias_f", [P, 2, D])
        bias_r = sb("bias_r", [P, 2, D])
        bias_s = sb("bias_s", [P, 2, D])
        bias_p = sb("bias_p", [P, 2, D], bf16)
        bias = sb("bias", [P, 2, TB, D], bf16)

        src_r = sb("src_r", [P, CH, P], i32)
        dst_r = sb("dst_r", [P, CH, P], i32)
        nxt_r = sb("nxt_r", [P, CH, P], i32)
        prv_r = sb("prv_r", [P, CH, P], i32)
        hi_r = sb("hi_r", [P, CH, P], i32)
        lo_r = sb("lo_r", [P, CH, P], i32)
        SRC, SCAT, SEG, RDEG, HI, LO = range(6)
        rows = [sb(f"rows{k}", [P, CH, P]) for k in range(6)]
        cols = [sb(f"cols{k}", [P, CH * P]) for k in range(6)]
        dst_f = sb("dst_f", [P, CH, P])
        nxt_f = sb("nxt_f", [P, CH, P])
        prv_f = sb("prv_f", [P, CH, P])
        new_f = sb("new_f", [P, CH, P])
        fst_f = sb("fst_f", [P, CH, P])
        seg_b = sb("seg_b", [P, CH, P], bf16)
        open_row = sb("open_row", [1, CH * P + 1])
        open_in = sb("open_in", [1, CH * P])
        open_col = sb("open_col", [P, CH])

        oh_hi = sb("oh_hi", [P, 2, TB, HIGH], f16)
        oh_lo = sb("oh_lo", [P, 2, TB, P], f16)
        cnt = sb("cnt", [P, HCH * P])
        tab = sb("tab", [P, HCH * P])

        gat_i = sb("gat_i", [P, 2, TB], i32)
        sca_i = sb("sca_i", [P, 2, TB], i32)
        rdg = sb("rdg", [P, 2, TB])
        ea = sb("ea", [P, 2, TB, ED])
        segq = sb("segq", [P, 2, W], bf16)
        xs = sb("xs", [P, 2, TB, D])
        ds = sb("ds", [P, 2, TB])
        eaT = sb("eaT", [ED, 2, W])
        he = sb("he", [P, 2, W])
        msg = sb("msg", [P, 2, TB, D])
        same = sb("same", [P, 2, TB, P])
        carry = sb("carry", [P, 2, TB, P])
        sums = sb("sums", [P, 2, D])
        scaled = sb("scaled", [P, 2, TB, D])

        xn = sb("xn", [P, XR, BN, D])
        ag = sb("ag", [P, XR, BN, D])
        on = sb("on", [P, 2, BN, D])
        comb = sb("comb", [P, 2, TB, D])
        cT = sb("cT", [P, 2, W])
        hn = sb("hn", [P, 2, W])
        res = sb("res", [P, 2, TB, D])
        rw = sb("rw", [P, 2, TB, D])
        yn = sb("yn", [P, 2, TB, D])
        squares = sb("squares", [P, 2, TB, D])
        ssq = sb("ssq", [P, 2, TB])
        rin = sb("rin", [P, 2, TB])
        rrt = sb("rrt", [P, 2, TB])
        st6 = sb("st6", [P, 2, TB, 6])
        mv = sb("mv", [P, 2, TB, 2])
        vin = sb("vin", [P, 2, TB])
        vrt = sb("vrt", [P, 2, TB])

        ps = [ctx.enter_context(nc.psum_tensor(f"bank{i}", [P, 512], f32)) for i in range(8)]

        zero_set = sem("zero_set")
        consts = sem("consts")
        ident_s = sem("ident_s")
        pads_set = sem("pads_set")
        rows_in = sem("rows_in")
        wts_in = sem("wts_in")
        agg_zeroed = sem("agg_zeroed")
        dchain = sem("dchain")
        achain = sem("achain")
        pchain = sem("pchain")
        lasts_ready = sem("lasts_ready")
        lasts_turned = sem("lasts_turned")
        open_scanned = sem("open_scanned")
        open_turned = sem("open_turned")
        len_ready = sem("len_ready")
        rdeg_ready = sem("rdeg_ready")
        rows_ready = sem("rows_ready")
        cols_turned = sem("cols_turned")
        cols_ready = sem("cols_ready")
        seg_out = sem("seg_out")
        onehot = sem("onehot")
        counted = sem("counted")
        cnt_ready = sem("cnt_ready")
        cnt_turned = sem("cnt_turned")
        tab_inv = sem("tab_inv")
        tab_ready = sem("tab_ready")
        tab_out = sem("tab_out")

        ea_in = sems("ea_in", 2)
        segq_in = sems("segq_in", 2)
        xs_in = sems("xs_in", 2)
        ds_in = sems("ds_in", 2)
        scattered = sems("scattered", 2)
        gidx_ready = sem("gidx_ready")
        sidx_ready = sem("sidx_ready")
        eaT_done = sem("eaT_done")
        eaT_ready = sem("eaT_ready")
        h_done = sem("h_done")
        h_ready = sem("h_ready")
        m_done = sem("m_done")
        msg_ready = sem("msg_ready")
        masks_ready = sem("masks_ready")
        tile_summed = sem("tile_summed")
        sums_ready = sem("sums_ready")
        scaled_ready = sem("scaled_ready")

        xn_in = sems("xn_in", XR)
        ag_in = sems("ag_in", XR)
        out_sent = sems("out_sent", 2)
        xe_ready = sem("xe_ready")
        comb_ready = sem("comb_ready")
        cT_done = sem("cT_done")
        cT_ready = sem("cT_ready")
        hn_done = sem("hn_done")
        hn_ready = sem("hn_ready")
        o_done = sem("o_done")
        res_ready = sem("res_ready")
        rw_ready = sem("rw_ready")
        ssq_ready = sem("ssq_ready")
        rin_ready = sem("rin_ready")
        rrt_ready = sem("rrt_ready")
        y_ready = sem("y_ready")
        vin_ready = sem("vin_ready")
        vrt_ready = sem("vrt_ready")
        fin_ready = sem("fin_ready")
        sp_passed = sem("sp_passed")
        pool_passed = sem("pool_passed")
        dve_passed = sem("dve_passed")
        pe_passed = sem("pe_passed")
        dve_a = sem("dve_a")
        dve_b = sem("dve_b")
        dve_c = sem("dve_c")
        dve_d = sem("dve_d")

        block = ctx.enter_context(nc.Block())

        def at(n):
            return n.value() if isinstance(n, Count) else n

        def need(eng, s, value):
            if not (isinstance(value, int) and value <= 0):
                eng.wait_ge(s, at(value))

        def apart(eng, passed):
            eng.sem_inc(passed, 1)

        def run(eng, total, unroll, step, tail=0, head=1, peel=0):
            rounds = total // unroll - peel
            for n in range(head * unroll):
                step(n, n % unroll)
            with eng.Fori(head, rounds) as i:
                for u in range(unroll):
                    step(Count(i, unroll, u), u)
            for n in range(rounds * unroll, total + tail):
                step(n, n % unroll)

        def live(n, total):
            return not isinstance(n, int) or 0 <= n < total

        def block_loads(B):
            return (B // XR + 1 + (isinstance(B, int) and B == BLOCKS - 1)) * 16

        ZERO_COLS = 32
        ZERO_DMAS = -(-NPP // ZERO_COLS) + 1

        ROW_DMAS = 13

        def index_rows(eng, tile, a, off):
            lo = 1 if off < 0 else 0
            n = 0
            if off < 0:
                eng.dma_start(tile[0:1, 0, 1:P], a[0:P - 1].rearrange("(o c) -> o c", o=1)).then_inc(rows_in, 16)
                eng.dma_start(tile[1:P, 0, :], a[P + off:P * P + off].rearrange("(p c) -> p c", c=P)).then_inc(rows_in, 16)
                n += 2
            span = P * P * (CH - 1)
            eng.dma_start(tile[:, lo:CH - 1, :],
                          a[lo * P * P + off:span + off].rearrange("(k p c) -> p k c", p=P, c=P)).then_inc(rows_in, 16)
            more = FULL - P * (CH - 1)
            eng.dma_start(tile[0:more, CH - 1, :],
                          a[span + off:FULL * P + off].rearrange("(p c) -> p c", c=P)).then_inc(rows_in, 16)
            eng.dma_start(tile[more:more + 1, CH - 1, 0:REST - off],
                          a[FULL * P + off:E].rearrange("(o c) -> o c", o=1)).then_inc(rows_in, 16)
            return n + 3

        x_main = x[0:NPP * P, :].rearrange("(p i) d -> p i d", p=P)
        ag_main = agg_d[0:NPP * P, :].rearrange("(p i) d -> p i d", p=P)
        out_main = out[0:NPP * P, :].rearrange("(p i) d -> p i d", p=P)

        @block.sync
        def _(sp):
            sp.wait_ge(pads_set, 4)
            sent = 0
            for tile, a, off in ((dst_r, dst, 0), (nxt_r, dst, 1), (prv_r, dst, -1), (src_r, src, 0)):
                sent += index_rows(sp, tile, a, off)
            assert 16 * sent == 16 * (ROW_DMAS + 1)
            for o, i in ((w1e[:, :], W1e), (w2e[:, :], W2e), (w1n[:, :], W1n), (w2n[:, :], W2n),
                         (b1e_c[:, :], b1e.rearrange("(p o) -> p o", o=1)),
                         (b1n_c[:, :], b1n.rearrange("(p o) -> p o", o=1)),
                         (rms_b[:, :], rms_w.rearrange("(o d) -> o d", o=1).partition_broadcast(P)),
                         (eps1[:, :], gin_eps.rearrange("(o d) -> o d", o=1).partition_broadcast(P)),
                         (bias_f[:, 0, :], b2e.rearrange("(o d) -> o d", o=1).partition_broadcast(P)),
                         (bias_f[:, 1, :], b2n.rearrange("(o d) -> o d", o=1).partition_broadcast(P))):
                sp.dma_start(o, i).then_inc(wts_in, 16)
            sp.wait_ge(rows_ready, 1)
            sp.dma_start(seg_d[:].rearrange("(k p c) -> p k c", p=P, c=P), seg_b[:, :, :]).then_inc(seg_out, 16)
            sp.wait_ge(seg_out, 16)

            def edge_loads(b, u):
                s = u % 2
                need(sp, eaT_done, b - 1)
                apart(sp, sp_passed)
                if isinstance(b, int) and b * W + W > E:
                    whole = FULL - b * TB
                    sp.dma_start(ea[:, s, 0:whole, :],
                                 edge_attr[b * W:FULL * P, :].rearrange("(j p) d -> p j d", p=P)).then_inc(ea_in[s], 16)
                    sp.dma_start(ea[0:REST, s, whole, :], edge_attr[FULL * P:E, :]).then_inc(ea_in[s], 16)
                else:
                    sp.dma_start(ea[:, s, :, :],
                                 edge_attr[bass.ds(at(b * W), W), :].rearrange("(j p) d -> p j d", p=P)).then_inc(ea_in[s], 16)
                need(sp, masks_ready, b - 1)
                apart(sp, sp_passed)
                sp.dma_start(segq[:, s, :],
                             seg_d[bass.ds(at(b * W), W)].rearrange("(o c) -> o c", o=1).partition_broadcast(P)
                             ).then_inc(segq_in[s], 16)

            run(sp, BATCHES, 2, edge_loads, peel=1)

            for s in range(2):
                sp.wait_ge(scattered[s], 16 * TB * (BATCHES // 2))

            def node_block(B, u):
                s = u % XR
                if live(B - 5, BLOCKS):
                    o = (u - 5) % 2
                    need(sp, fin_ready, (B - 5) * 2 + 2)
                    if isinstance(B, int) and B - 5 == BLOCKS - 1:
                        sp.dma_start(out_main[:, (B - 5) * BN:NPP, :], on[:, o, 0:LASTC, :]).then_inc(out_sent[o], 16)
                        sp.dma_start(out[NPP * P:N, :], on[0:NREM, o, LASTC, :]).then_inc(out_sent[o], 16)
                    else:
                        sp.dma_start(out_main[:, bass.ds(at((B - 5) * BN), BN), :], on[:, o, :, :]).then_inc(out_sent[o], 16)
                if live(B, BLOCKS):
                    need(sp, y_ready, B * 2 - (2 * XR - 2))
                    need(sp, comb_ready, B * 2 - (2 * XR - 2))
                    for t, d, view, s_in in ((xn, x, x_main, xn_in), (ag, agg_d, ag_main, ag_in)):
                        if isinstance(B, int) and B == BLOCKS - 1:
                            sp.dma_start(t[:, s, 0:LASTC, :], view[:, B * BN:NPP, :]).then_inc(s_in[s], 16)
                            sp.dma_start(t[0:NREM, s, LASTC, :], d[NPP * P:N, :]).then_inc(s_in[s], 16)
                        else:
                            sp.dma_start(t[:, s, :, :], view[:, bass.ds(at(B * BN), BN), :]).then_inc(s_in[s], 16)

            run(sp, BLOCKS, XR, node_block, tail=5, head=2)
            for o in range(2):
                blocks = len(range(o, BLOCKS, 2))
                sp.wait_ge(out_sent[o], 16 * (blocks + int((BLOCKS - 1) % 2 == o)))

        @block.gpsimd
        def _(pool):
            pool.memset(zeros[:, :], 0.0).then_inc(zero_set, 1)
            for t, v in ((dst_r, NO_NODE), (nxt_r, NO_NODE), (prv_r, NO_NODE), (src_r, 0)):
                pool.memset(t[:, :, :], v).then_inc(pads_set, 1)
            pool.memset(ident[:, :], 0.0).then_inc(pchain, 1)
            pool.wait_ge(pchain, 1)
            pool.affine_select(out=ident[:, :], in_=ident[:, :], compare_op=ALU.not_equal, fill=1.0, base=0,
                               pattern=[[-1, P]], channel_multiplier=1).then_inc(ident_s, 1)
            pool.iota(iota_i[:, :], pattern=[[1, HIGH]], base=0, channel_multiplier=0).then_inc(consts, 1)
            pool.iota(gidx_i[:, :, :], pattern=[[P * P, CH], [1, P]], base=0, channel_multiplier=P).then_inc(consts, 1)
            pool.memset(ones[:, :], 1.0).then_inc(consts, 1)
            pool.memset(ones_b[:, :], 1.0).then_inc(consts, 1)
            pool.memset(cnt[:, :], 0.0).then_inc(consts, 1)
            pool.memset(ea[:, :, :, :], 0.0).then_inc(consts, 1)

            def gathers(b, u):
                s = u % 2
                if live(b, BATCHES):
                    pool.wait_ge(gidx_ready, at(b + 1))
                    need(pool, msg_ready, b - 1)
                    apart(pool, pool_passed)
                    for j in range(TB):
                        pool.indirect_dma_start(out=xs[:, s, j, :], out_offset=None, in_=x,
                                                in_offset=bass.IndirectOffsetOnAxis(ap=gat_i[:, s, j:j + 1], axis=0)
                                                ).then_inc(xs_in[s], 16)
                    if isinstance(b, int) and b == 0:
                        pool.wait_ge(tab_out, 16)
                    need(pool, masks_ready, b - 1)
                    apart(pool, pool_passed)
                    for j in range(TB):
                        pool.indirect_dma_start(out=ds[:, s, j:j + 1], out_offset=None, in_=tab_rows,
                                                in_offset=bass.IndirectOffsetOnAxis(ap=gat_i[:, s, j:j + 1], axis=0)
                                                ).then_inc(ds_in[s], 16)
                c = b - 2
                if live(c, BATCHES):
                    if isinstance(c, int) and c == 0:
                        pool.wait_ge(agg_zeroed, ZERO_DMAS * 16)
                    pool.wait_ge(sidx_ready, at(c + 1))
                    for j in range(TB):
                        pool.wait_ge(scaled_ready, at(c * TB + j + 1))
                        apart(pool, pool_passed)
                        pool.indirect_dma_start(out=agg_rows,
                                                out_offset=bass.IndirectOffsetOnAxis(ap=sca_i[:, s, j:j + 1], axis=0),
                                                in_=scaled[:, s, j, :], in_offset=None,
                                                bounds_check=N - 1, oob_is_err=False).then_inc(scattered[s], 16)

            run(pool, BATCHES, 2, gathers, tail=2)

            def node_step(n, u):
                if live(n, STEPS):
                    s, xsl, h = u % 2, (u // 2) % XR, (u % 2) * TB
                    B = (n) // 2
                    loads = block_loads(B)
                    pool.wait_ge(xn_in[xsl], at(loads))
                    pool.wait_ge(ag_in[xsl], at(loads))
                    need(pool, cT_done, n - 1)
                    apart(pool, pool_passed)
                    pool.tensor_scalar(comb[:, s, :, :], xn[:, xsl, h:h + TB, :], eps1[:, 0:1], None,
                                       ALU.mult).then_inc(xe_ready, 1)
                    pool.wait_ge(xe_ready, at(n + 1))
                    pool.tensor_tensor(comb[:, s, :, :], comb[:, s, :, :], ag[:, xsl, h:h + TB, :],
                                       ALU.add).then_inc(comb_ready, 1)
                m, s = n - 3, (u - 3) % 2
                if live(m, STEPS):
                    pool.wait_ge(res_ready, at(m + 1))
                    need(pool, y_ready, m - 1)
                    pool.tensor_tensor(rw[:, s, :, :], res[:, s, :, :],
                                       rms_b[:, :].unsqueeze(1).to_broadcast([P, TB, D]), ALU.mult).then_inc(rw_ready, 1)

            run(pool, STEPS, 2 * XR, node_step, tail=3)

        @block.scalar
        def _(act):
            act.wait_ge(zero_set, 1)
            for c in range(0, NPP, ZERO_COLS):
                w = min(ZERO_COLS, NPP - c)
                act.dma_start(ag_main[:, c:c + w, :],
                              zeros[:, 0:w * D].rearrange("p (i d) -> p i d", d=D)).then_inc(agg_zeroed, 16)
            act.dma_start(agg_d[NPP * P:N, :], zeros[0:NREM, 0:D]).then_inc(agg_zeroed, 16)

            act.wait_ge(len_ready, 1)
            act.activation(rows[RDEG][:, :, :], rows[RDEG][:, :, :], ACT.Sqrt).then_inc(rdeg_ready, 1)
            for k in range(6):
                act.wait_ge(cols_turned, k + 1)
                act.activation(cols[k][:, :], ps[4 + k % 2][:, :], ACT.Copy).then_inc(cols_ready, 1)
            act.wait_ge(tab_inv, 1)
            act.activation(tab[:, :], tab[:, :], ACT.Sqrt).then_inc(tab_ready, 1)
            act.wait_ge(tab_ready, 1)
            act.dma_start(tab_d[:, :].rearrange("(c p l) o -> p c (l o)", p=P, l=P),
                          tab[:, :].rearrange("p (c l) -> p c l", l=P)).then_inc(tab_out, 16)

            def tile_out(b, u, j):
                s = u % 2
                t = b * TB + j
                act.wait_ge(tile_summed, at(t + 1))
                act.activation(sums[:, j % 2, :], ps[6 + j % 2][:, 0:D], ACT.Copy).then_inc(sums_ready, 1)
                if j == 0:
                    act.wait_ge(sidx_ready, at(b + 1))
                    need(act, scattered[s], b // 2 * 16 * TB)
                act.activation(scaled[:, s, j, :], ps[6 + j % 2][:, 0:D], ACT.Copy,
                               scale=rdg[:, s, j:j + 1]).then_inc(scaled_ready, 1)

            def edge_step(b, u):
                s = u % 2
                if live(b, BATCHES):
                    act.wait_ge(eaT_done, at(b + 1))
                    need(act, h_done, b - 1)
                    act.activation(eaT[:, s, :], ps[2][0:ED, :], ACT.Copy).then_inc(eaT_ready, 1)
                if live(b - 1, BATCHES):
                    tile_out(b - 1, u - 1, 0)
                if live(b, BATCHES):
                    act.wait_ge(h_done, at(b + 1))
                    need(act, m_done, b - 1)
                    act.activation(he[:, s, :], ps[3][:, :], ACT.Relu, bias=b1e_c[:, 0:1]).then_inc(h_ready, 1)
                if live(b - 1, BATCHES):
                    for j in range(1, TB):
                        tile_out(b - 1, u - 1, j)

            act.wait_ge(wts_in, 160)
            run(act, BATCHES, 2, edge_step, tail=1)

            def node_step(n, u):
                s = u % 2
                if live(n, STEPS):
                    act.wait_ge(cT_done, at(n + 1))
                    need(act, hn_done, n - 1)
                    act.activation(cT[:, s, :], ps[s][:, :], ACT.Copy).then_inc(cT_ready, 1)
                m, s = n - 1, (u - 1) % 2
                if live(m, STEPS):
                    act.wait_ge(hn_done, at(m + 1))
                    need(act, o_done, m - 1)
                    act.activation(hn[:, s, :], ps[2 + s][:, :], ACT.Relu, bias=b1n_c[:, 0:1]).then_inc(hn_ready, 1)
                m, s = n - 3, (u - 3) % 2
                if live(m, STEPS):
                    act.wait_ge(res_ready, at(m + 1))
                    need(act, rin_ready, m - 1)
                    for j in range(TB):
                        act.activation(squares[:, s, j, :], res[:, s, j, :], ACT.Square,
                                       accum_out=ssq[:, s, j:j + 1]).then_inc(ssq_ready, 1)
                m, s = n - 4, (u - 4) % 2
                if live(m, STEPS):
                    act.wait_ge(rin_ready, at(m + 1))
                    need(act, y_ready, m - 1)
                    act.activation(rrt[:, s, :], rin[:, s, :], ACT.Sqrt).then_inc(rrt_ready, 1)
                m, s = n - 5, (u - 5) % 2
                if live(m, STEPS):
                    act.wait_ge(vin_ready, at(m + 1))
                    need(act, fin_ready, m - 1)
                    act.activation(vrt[:, s, :], vin[:, s, :], ACT.Sqrt).then_inc(vrt_ready, 1)

            run(act, STEPS, 2 * XR, node_step, tail=6)

        @block.vector
        def _(dve):
            done = [0]

            def link(ins):
                done[0] += 1
                ins.then_inc(dchain, 1)
                dve.wait_ge(dchain, done[0])

            dve.wait_ge(consts, 6)
            dve.tensor_copy(iota_h[:, :], iota_i[:, :])
            link(dve.tensor_copy(gidx[:, :, :], gidx_i[:, :, :]))
            dve.wait_ge(rows_in, 16 * (ROW_DMAS + 1))
            dve.tensor_copy(dst_f[:, :, :], dst_r[:, :, :])
            dve.tensor_copy(nxt_f[:, :, :], nxt_r[:, :, :])
            dve.tensor_scalar(hi_r[:, :, :], dst_r[:, :, :], 7, None, ALU.arith_shift_right)
            dve.tensor_scalar(lo_r[:, :, :], dst_r[:, :, :], P - 1, None, ALU.bitwise_and)
            dve.tensor_copy(rows[SRC][:, :, :], src_r[:, :, :])
            link(dve.tensor_copy(prv_f[:, :, :], prv_r[:, :, :]))
            dve.tensor_copy(rows[HI][:, :, :], hi_r[:, :, :])
            dve.tensor_copy(rows[LO][:, :, :], lo_r[:, :, :])
            dve.tensor_tensor(nxt_f[:, :, :], dst_f[:, :, :], nxt_f[:, :, :], ALU.is_equal)
            link(dve.tensor_tensor(new_f[:, :, :], dst_f[:, :, :], prv_f[:, :, :], ALU.not_equal))
            dve.scalar_tensor_tensor(rows[SCAT][:, :, :], nxt_f[:, :, :], SKIP, dst_f[:, :, :], ALU.mult, ALU.add)
            link(dve.scalar_tensor_tensor(fst_f[:, :, :], gidx[:, :, :], 1.0, new_f[:, :, :], ALU.add, ALU.mult))
            for k in range(CH):
                dve.tensor_tensor_scan(rows[SEG][:, k, :], ones[:, :], new_f[:, k, :], 0.0, ALU.mult, ALU.add)
                last = dve.tensor_tensor_scan(prv_f[:, k, :], ones[:, :], fst_f[:, k, :], 0.0, ALU.mult, ALU.max)
            link(last)
            last = dve.tensor_copy(seg_b[:, :, :], rows[SEG][:, :, :])
            dve.tensor_copy(open_col[:, :], prv_f[:, :, P - 1]).then_inc(lasts_ready, 1)
            link(last)
            dve.memset(open_row[:, 0:1], 0.0)
            dve.wait_ge(lasts_turned, 1)
            link(dve.tensor_copy(open_in[:, :], ps[4][0:1, :]))
            link(dve.tensor_tensor_scan(open_row[:, 1:CH * P + 1], open_in[:, :], open_in[:, :], 0.0,
                                        ALU.max, ALU.max))
            dve.sem_inc(open_scanned, 1)
            dve.wait_ge(open_turned, 1)
            link(dve.tensor_copy(open_col[:, :], ps[5][:, 0:CH]))
            for k in range(CH):
                last = dve.tensor_scalar(fst_f[:, k, :], prv_f[:, k, :], open_col[:, k:k + 1], None, ALU.max)
            link(last)
            link(dve.scalar_tensor_tensor(new_f[:, :, :], fst_f[:, :, :], -1.0, gidx[:, :, :], ALU.mult, ALU.add))
            link(dve.tensor_scalar(new_f[:, :, :], new_f[:, :, :], 2.0, None, ALU.add))
            dve.reciprocal(rows[RDEG][:, :, :], new_f[:, :, :]).then_inc(len_ready, 1)
            dve.sem_inc(rows_ready, 1)

            dve.wait_ge(wts_in, 160)
            link(dve.tensor_scalar(eps1[:, :], eps1[:, :], 1.0, None, ALU.add))
            dve.wait_ge(ident_s, 1)
            for k in range(3):
                link(dve.tensor_copy(bias_p[:, :, :], bias_f[:, :, :]))
                link(dve.tensor_copy(bias_r[:, :, :], bias_p[:, :, :]))
                if k == 0:
                    link(dve.tensor_scalar(bias_s[:, :, :], bias_r[:, :, :], ident[:, k:k + 1], None, ALU.mult))
                else:
                    link(dve.scalar_tensor_tensor(bias_s[:, :, :], bias_r[:, :, :], ident[:, k:k + 1],
                                                  bias_s[:, :, :], ALU.mult, ALU.add))
                link(dve.tensor_tensor(bias_f[:, :, :], bias_f[:, :, :], bias_r[:, :, :], ALU.subtract))
            for j in range(TB):
                last = dve.tensor_copy(bias[:, :, j, :], bias_s[:, :, :])
            link(last)

            dve.wait_ge(cols_ready, 6)

            def count_step(b, u):
                s = u % 2
                need(dve, counted, b - 1)
                for j in range(TB):
                    dve.tensor_scalar(oh_hi[:, s, j, :], iota_h[:, :], cols[HI][:, bass.ds(at(b * TB + j), 1)], None,
                                      ALU.is_equal)
                    dve.tensor_scalar(oh_lo[:, s, j, :], iota_h[:, 0:P], cols[LO][:, bass.ds(at(b * TB + j), 1)], None,
                                      ALU.is_equal).then_inc(onehot, 1)

            run(dve, BATCHES, 2, count_step)
            dve.wait_ge(counted, BATCHES)
            dve.tensor_copy(cnt[:, 0:512], ps[0][:, :])
            dve.tensor_copy(cnt[:, 512:HIGH], ps[1][:, 0:HIGH - 512]).then_inc(cnt_ready, 1)
            dve.wait_ge(cnt_turned, 1)
            dve.tensor_scalar(tab[:, 0:512], ps[4][:, :], 1.0, None, ALU.max)
            link(dve.tensor_scalar(tab[:, 512:HCH * P], ps[5][:, 0:HCH * P - 512], 1.0, None, ALU.max))
            dve.reciprocal(tab[:, :], tab[:, :]).then_inc(tab_inv, 1)

            def gather_indices(b, u):
                dve.tensor_copy(gat_i[:, u % 2, :], cols[SRC][:, bass.ds(at(b * TB), TB)]).then_inc(gidx_ready, 1)

            def edge_step(b, u):
                s = u % 2
                if live(b + 1, BATCHES):
                    need(dve, xs_in[1 - s], (b + 1) // 2 * 16 * TB)
                    need(dve, ds_in[1 - s], (b + 1) // 2 * 16 * TB)
                    gather_indices(b + 1, u + 1)
                need(dve, scattered[s], b // 2 * 16 * TB)
                dve.tensor_copy(sca_i[:, s, :], cols[SCAT][:, bass.ds(at(b * TB), TB)])
                dve.tensor_copy(rdg[:, s, :], cols[RDEG][:, bass.ds(at(b * TB), TB)]).then_inc(sidx_ready, 1)
                dve.wait_ge(segq_in[s], at((b // 2 + 1) * 16))
                need(dve, tile_summed, (b - 1) * TB)
                dve.tensor_scalar(carry[:, s, :, :].rearrange("p j c -> p (j c)"), segq[:, s, :], 0.0,
                                  ident[:, P - 1:P], ALU.is_equal, ALU.mult)
                dve.wait_ge(ds_in[s], at((b // 2 + 1) * 16 * TB))
                for j in range(TB):
                    last = dve.tensor_scalar(same[:, s, j, :], segq[:, s, j * P:(j + 1) * P],
                                             cols[SEG][:, bass.ds(at(b * TB + j), 1)], ds[:, s, j:j + 1],
                                             ALU.is_equal, ALU.mult)
                last.then_inc(masks_ready, 1)
                dve.wait_ge(xs_in[s], at((b // 2 + 1) * 16 * TB))
                dve.wait_ge(m_done, at(b + 1))
                dve.tensor_tensor(msg[:, s, :, :].rearrange("p j d -> p (j d)"), ps[4 + s][:, :],
                                  xs[:, s, :, :].rearrange("p j d -> p (j d)"), ALU.add).then_inc(msg_ready, 1)

            gather_indices(0, 0)
            run(dve, BATCHES, 2, edge_step, peel=1)

            def node_step(n, u):
                m, s = n - 4, (u - 4) % 2
                if live(m, STEPS):
                    dve.wait_ge(ssq_ready, at(m * TB + TB))
                    need(dve, rrt_ready, m - 1)
                    dve.tensor_scalar(rin[:, s, :], ssq[:, s, :], 1.0 / D, RMS_EPS, ALU.mult, ALU.add
                                      ).then_inc(dve_a, 1)
                    dve.wait_ge(dve_a, at(m + 1))
                    dve.reciprocal(rin[:, s, :], rin[:, s, :]).then_inc(rin_ready, 1)
                m, s = n - 2, (u - 2) % 2
                if live(m, STEPS):
                    xsl, h = ((u - 2) // 2) % XR, ((u - 2) % 2) * TB
                    dve.wait_ge(o_done, at(m + 1))
                    need(dve, ssq_ready, (m - 1) * TB)
                    need(dve, rw_ready, m - 1)
                    dve.tensor_tensor(res[:, s, :, :].rearrange("p j d -> p (j d)"), ps[4 + s][:, :],
                                      xn[:, xsl, h:h + TB, :].rearrange("p j d -> p (j d)"),
                                      ALU.add).then_inc(res_ready, 1)
                m, s = n - 5, (u - 5) % 2
                if live(m, STEPS):
                    xsl, h = ((u - 5) // 2) % XR, ((u - 5) % 2) * TB
                    dve.wait_ge(rrt_ready, at(m + 1))
                    dve.wait_ge(rw_ready, at(m + 1))
                    need(dve, fin_ready, m - 1)
                    for j in range(TB):
                        last = dve.scalar_tensor_tensor(yn[:, s, j, :], rw[:, s, j, :], rrt[:, s, j:j + 1],
                                                        xn[:, xsl, h + j, :], ALU.mult, ALU.add)
                    last.then_inc(y_ready, 1)
                    dve.wait_ge(y_ready, at(m + 1))
                    for j in range(TB):
                        last = dve.bn_stats(st6[:, s, j, :], yn[:, s, j, :])
                    last.then_inc(dve_b, 1)
                    dve.wait_ge(dve_b, at(m + 1))
                    apart(dve, dve_passed)
                    for j in range(TB):
                        last = dve.bn_aggr(mv[:, s, j, :], st6[:, s, j, :])
                    last.then_inc(dve_c, 1)
                    dve.wait_ge(dve_c, at(m + 1))
                    need(dve, vrt_ready, m - 1)
                    dve.tensor_scalar(vin[:, s, :], mv[:, s, :, 1], LN_EPS, None, ALU.add).then_inc(dve_d, 1)
                    dve.wait_ge(dve_d, at(m + 1))
                    dve.reciprocal(vin[:, s, :], vin[:, s, :]).then_inc(vin_ready, 1)
                m, s = n - 6, (u - 6) % 2
                if live(m, STEPS):
                    B = (m) // 2
                    o, h = ((u - 6) // 2) % 2, ((u - 6) % 2) * TB
                    dve.wait_ge(vrt_ready, at(m + 1))
                    if (u - 6) % 2 == 0:
                        need(dve, out_sent[o], B // 2 * 16)
                    for j in range(TB):
                        last = dve.tensor_scalar(on[:, o, h + j, :], yn[:, s, j, :], mv[:, s, j, 0:1],
                                                 vrt[:, s, j:j + 1], ALU.subtract, ALU.mult)
                    last.then_inc(fin_ready, 1)

            run(dve, STEPS, 2 * XR, node_step, tail=6)

        @block.tensor
        def _(pe):
            pe.wait_ge(ident_s, 1)
            pe.wait_ge(consts, 6)
            pe.wait_ge(lasts_ready, 1)
            for k in range(CH):
                last = pe.transpose(ps[4][0:1, k * P:(k + 1) * P], open_col[:, k:k + 1], ident[:, :])
            last.then_inc(lasts_turned, 1)
            pe.wait_ge(open_scanned, 1)
            for k in range(CH):
                last = pe.transpose(ps[5][:, k:k + 1], open_row[0:1, k * P:(k + 1) * P], ident[0:1, 0:1])
            last.then_inc(open_turned, 1)
            pe.wait_ge(rows_ready, 1)
            pe.wait_ge(rdeg_ready, 1)
            for k in range(6):
                need(pe, cols_ready, k - 1)
                for c in range(CH):
                    last = pe.transpose(ps[4 + k % 2][:, c * P:(c + 1) * P], rows[k][:, c, :], ident[:, :])
                last.then_inc(cols_turned, 1)

            def count_step(b, u):
                s = u % 2
                for j in range(TB):
                    pe.wait_ge(onehot, at(b * TB + j + 1))
                    first = isinstance(b, int) and b == 0 and j == 0
                    end = isinstance(b, int) and b == BATCHES - 1 and j == TB - 1
                    pe.matmul(ps[0][:, :], oh_lo[:, s, j, :], oh_hi[:, s, j, 0:512], start=first, stop=end)
                    last = pe.matmul(ps[1][:, 0:HIGH - 512], oh_lo[:, s, j, :], oh_hi[:, s, j, 512:HIGH],
                                     start=first, stop=end)
                last.then_inc(counted, 1)

            run(pe, BATCHES, 2, count_step, peel=1)
            pe.wait_ge(cnt_ready, 1)
            pe.wait_ge(cols_ready, 6)
            for c in range(HCH):
                last = pe.transpose(ps[4 + c // 4][:, (c % 4) * P:(c % 4 + 1) * P], cnt[:, c * P:(c + 1) * P],
                                    ident[:, :])
            last.then_inc(cnt_turned, 1)

            pe.wait_ge(wts_in, 160)
            pe.wait_ge(tab_inv, 1)

            def tile_sum(b, u, j):
                s = u % 2
                t = b * TB + j
                if j == 0:
                    pe.wait_ge(msg_ready, at(b + 1))
                    pe.wait_ge(masks_ready, at(b + 1))
                need(pe, scaled_ready, t - 1)
                first = isinstance(t, int) and t == 0
                last = pe.matmul(ps[6 + j % 2][:, 0:D], same[:, s, j, :], msg[:, s, j, :], start=True, stop=first)
                if not first:
                    pe.wait_ge(sums_ready, at(t))
                    last = pe.matmul(ps[6 + j % 2][:, 0:D], carry[:, s, j, :], sums[:, (j - 1) % 2, :],
                                     start=False, stop=True)
                last.then_inc(tile_summed, 1)

            def edge_step(b, u):
                s = u % 2
                if live(b, BATCHES):
                    loads = (b // 2 + 1) * 16 + (16 if isinstance(b, int) and b * W + W > E else 0)
                    pe.wait_ge(ea_in[s], at(loads))
                    need(pe, eaT_ready, b)
                    apart(pe, pe_passed)
                    for j in range(TB):
                        last = pe.transpose(ps[2][0:ED, j * P:(j + 1) * P], ea[:, s, j, :], ident[:, :])
                    last.then_inc(eaT_done, 1)
                if live(b - 1, BATCHES):
                    tile_sum(b - 1, u - 1, 0)
                if live(b, BATCHES):
                    pe.wait_ge(eaT_ready, at(b + 1))
                    need(pe, h_ready, b)
                    pe.matmul(ps[3][:, :], w1e[:, :], eaT[:, s, :], start=True, stop=True).then_inc(h_done, 1)
                if live(b - 1, BATCHES):
                    tile_sum(b - 1, u - 1, 1)
                if live(b, BATCHES):
                    need(pe, msg_ready, b - 1)
                    pe.matmul(ps[4 + s][:, :], ones_b[:, :], bias[:, 0, :, :].rearrange("p j d -> p (j d)"),
                              start=True, stop=False)
                    pe.wait_ge(h_ready, at(b + 1))
                    for j in range(TB):
                        last = pe.matmul(ps[4 + s][:, j * P:(j + 1) * P], he[:, s, j * P:(j + 1) * P], w2e[:, :],
                                         start=False, stop=j == TB - 1)
                    last.then_inc(m_done, 1)
                if live(b - 1, BATCHES):
                    tile_sum(b - 1, u - 1, 2)
                    tile_sum(b - 1, u - 1, 3)

            run(pe, BATCHES, 2, edge_step, tail=1, peel=1)

            def node_step(n, u):
                s = u % 2
                if live(n, STEPS):
                    pe.wait_ge(comb_ready, at(n + 1))
                    need(pe, cT_ready, n - 1)
                    for j in range(TB):
                        last = pe.transpose(ps[s][:, j * P:(j + 1) * P], comb[:, s, j, :], ident[:, :])
                    last.then_inc(cT_done, 1)
                m, s = n - 1, (u - 1) % 2
                if live(m, STEPS):
                    pe.wait_ge(cT_ready, at(m + 1))
                    need(pe, hn_ready, m - 1)
                    pe.matmul(ps[2 + s][:, :], w1n[:, :], cT[:, s, :], start=True, stop=True).then_inc(hn_done, 1)
                m, s = n - 2, (u - 2) % 2
                if live(m, STEPS):
                    need(pe, res_ready, m - 1)
                    pe.matmul(ps[4 + s][:, :], ones_b[:, :], bias[:, 1, :, :].rearrange("p j d -> p (j d)"),
                              start=True, stop=False)
                    pe.wait_ge(hn_ready, at(m + 1))
                    for j in range(TB):
                        last = pe.matmul(ps[4 + s][:, j * P:(j + 1) * P], hn[:, s, j * P:(j + 1) * P], w2n[:, :],
                                         start=False, stop=j == TB - 1)
                    last.then_inc(o_done, 1)

            run(pe, STEPS, 2 * XR, node_step, tail=2)


_INS = ['x', 'src', 'dst', 'edge_attr_64', 'L0_gnn_W1n', 'L0_gnn_b1n', 'L0_gnn_W2n', 'L0_gnn_b2n', 'L0_gnn_W1e',
        'L0_gnn_b1e', 'L0_gnn_W2e', 'L0_gnn_b2e', 'L0_gnn_gin_eps', 'L0_gnn_rms_w']


def kernel(**inputs):
    import numpy as _np
    import concourse.bacc as _bacc
    from concourse import mybir as _mybir
    from concourse.bass_utils import run_bass_kernel_spmd as _run

    nc = _bacc.Bacc("TRN2", target_bir_lowering=False, num_devices=1)
    arrays, args = {}, []
    for name in _INS:
        a = _np.asarray(inputs[name])
        a = _np.ascontiguousarray(a.reshape(a.shape or (1,)))
        arrays[f"in_{name}"] = a
        args.append(nc.dram_tensor(f"in_{name}", a.shape, _mybir.dt.from_np(a.dtype), kind="ExternalInput").ap())
    out = nc.dram_tensor("out_0", arrays["in_x"].shape, _mybir.dt.float32, kind="ExternalOutput").ap()
    build(nc, *args, out)
    r = _run(nc, [arrays], core_ids=[0])
    return r.results[0]["out_0"]
```

```python
import concourse.bass as bass
from concourse import mybir
from contextlib import ExitStack


class Count:

    def __init__(self, i, per, base):
        self.i, self.per, self.base = i, per, base

    def __add__(self, k):
        return Count(self.i, self.per, self.base + k)

    def __sub__(self, k):
        return Count(self.i, self.per, self.base - k)

    def __mul__(self, k):
        return Count(self.i, self.per * k, self.base * k)

    def __floordiv__(self, k):
        assert self.per % k == 0
        return Count(self.i, self.per // k, self.base // k)

    def value(self):
        return self.i * self.per + self.base if self.base >= 0 else self.i * self.per - -self.base


def build(nc, x, src, dst, edge_attr, W1n, b1n, W2n, b2n, W1e, b1e, W2e, b2e, gin_eps, rms_w, out):
    f32 = mybir.dt.float32
    bf16 = mybir.dt.bfloat16
    f16 = mybir.dt.float16
    i32 = mybir.dt.int32
    ALU = mybir.AluOpType
    ACT = mybir.ActivationFunctionType

    P = 128
    N, D = x.shape
    E, ED = edge_attr.shape
    RMS_EPS = 1.1920929e-07
    LN_EPS = 1e-05

    TB = 4
    W = TB * P
    TILES = -(-E // P)
    BATCHES = -(-TILES // TB)
    BATCHES += BATCHES % 2
    FULL = E // P
    REST = E - FULL * P
    CH = TB
    assert BATCHES * TB <= CH * P and FULL // P == CH - 1
    NO_NODE = 2 * N
    SKIP = 1000000.0

    HIGH = -(-N // P)
    HIGH += HIGH % 2
    HCH = -(-HIGH // P)

    NPP = N // P
    NREM = N - NPP * P
    BN = 16
    SPB = BN // TB
    BLOCKS = -(-(NPP + 1) // BN)
    LASTC = NPP - (BLOCKS - 1) * BN
    assert 0 < LASTC < BN
    STEPS = SPB * BLOCKS
    XR = 4

    agg_d = nc.dram_tensor("agg_scratch", (N, D), f32)
    tab_d = nc.dram_tensor("rsqrt_degree_scratch", (HCH * P * P, 1), f32)
    seg_d = nc.dram_tensor("segment_number_scratch", (CH * P * P,), bf16)
    agg_rows = agg_d[:, :]
    tab_rows = tab_d[:, :]

    with ExitStack() as ctx:
        def sb(name, shape, dt=f32):
            return ctx.enter_context(nc.sbuf_tensor(name, shape, dt))

        def sem(name):
            return ctx.enter_context(nc.semaphore(name))

        def sems(name, n):
            return [sem(f"{name}{i}") for i in range(n)]

        ident = sb("ident", [P, P])
        iota_i = sb("iota_i", [P, HIGH], i32)
        iota_h = sb("iota_h", [P, HIGH], f16)
        gidx_i = sb("gidx_i", [P, CH, P], i32)
        gidx = sb("gidx", [P, CH, P])
        ones = sb("ones", [P, P])
        ones_b = sb("ones_b", [P, P], bf16)
        on = sb("on", [P, 2, BN, D])
        w1e = sb("w1e", [ED, D])
        w2e = sb("w2e", [D, D])
        w1n = sb("w1n", [D, D])
        w2n = sb("w2n", [D, D])
        b1e_c = sb("b1e_c", [D, 1])
        b1n_c = sb("b1n_c", [D, 1])
        rms_b = sb("rms_b", [P, D])
        eps1 = sb("eps1", [P, 1])
        bias_f = sb("bias_f", [P, 2, D])
        bias_r = sb("bias_r", [P, 2, D])
        bias_s = sb("bias_s", [P, 2, D])
        bias_p = sb("bias_p", [P, 2, D], bf16)
        bias = sb("bias", [P, 2, TB, D], bf16)

        persistent, early = ctx, ctx.enter_context(ExitStack())

        def sb(name, shape, dt=f32):
            return early.enter_context(nc.sbuf_tensor(name, shape, dt))

        src_r = sb("src_r", [P, CH, P], i32)
        dst_r = sb("dst_r", [P, CH, P], i32)
        nxt_r = sb("nxt_r", [P, CH, P], i32)
        prv_r = sb("prv_r", [P, CH, P], i32)
        hi_r = sb("hi_r", [P, CH, P], i32)
        lo_r = sb("lo_r", [P, CH, P], i32)
        SRC, SCAT, SEG, RDEG, HI, LO = range(6)
        rows = [sb(f"rows{k}", [P, CH, P]) for k in range(6)]
        cols = [sb(f"cols{k}", [P, CH * P]) for k in range(6)]
        dst_f = sb("dst_f", [P, CH, P])
        nxt_f = sb("nxt_f", [P, CH, P])
        prv_f = sb("prv_f", [P, CH, P])
        new_f = sb("new_f", [P, CH, P])
        fst_f = sb("fst_f", [P, CH, P])
        seg_b = sb("seg_b", [P, CH, P], bf16)
        open_row = sb("open_row", [1, CH * P + 1])
        open_in = sb("open_in", [1, CH * P])
        open_col = sb("open_col", [P, CH])

        oh_hi = sb("oh_hi", [P, 2, TB, HIGH], f16)
        oh_lo = sb("oh_lo", [P, 2, TB, P], f16)
        cnt = sb("cnt", [P, HCH * P])
        tab = sb("tab", [P, HCH * P])

        gat_i = sb("gat_i", [P, 2, TB], i32)
        sca_i = sb("sca_i", [P, 2, TB], i32)
        rdg = sb("rdg", [P, 2, TB])
        ea = sb("ea", [P, 2, TB, ED])
        segq = sb("segq", [P, 2, W], bf16)
        xs = sb("xs", [P, 2, TB, D])
        ds = sb("ds", [P, 2, TB])
        eaT = sb("eaT", [ED, 2, W])
        he = sb("he", [P, 2, W])
        msg = sb("msg", [P, 2, TB, D])
        same = sb("same", [P, 2, TB, P])
        carry = sb("carry", [P, 2, TB, P])
        sums = sb("sums", [P, 2, D])
        scaled = sb("scaled", [P, 2, TB, D])

        early.close()

        def sb(name, shape, dt=f32):
            return persistent.enter_context(nc.sbuf_tensor(name, shape, dt))

        xn = sb("xn", [P, XR, BN, D])
        ag = sb("ag", [P, XR, BN, D])
        xe = sb("xe", [P, 2, TB, D])
        comb = sb("comb", [P, 2, TB, D])
        cT = sb("cT", [P, 2, W])
        hn = sb("hn", [P, 2, W])
        res = sb("res", [P, 2, TB, D])
        rw = sb("rw", [P, 4, TB, D])
        yn = sb("yn", [P, 4, TB, D])
        squares = sb("squares", [P, 2, TB, D])
        ssq = sb("ssq", [P, 2, TB])
        rin = sb("rin", [P, 2, TB])
        rrt = sb("rrt", [P, 2, TB])
        ysum = sb("ysum", [P, 2, TB])
        neg_mean = sb("neg_mean", [P, 4, TB])
        deviations = sb("deviations", [P, 2, TB, D])
        var_sum = sb("var_sum", [P, 2, TB])
        vin = sb("vin", [P, 2, TB])
        vrt = sb("vrt", [P, 2, TB])

        ps = [ctx.enter_context(nc.psum_tensor(f"bank{i}", [P, 512], f32)) for i in range(8)]

        zero_set = sem("zero_set")
        consts = sem("consts")
        ident_s = sem("ident_s")
        pads_set = sem("pads_set")
        rows_in = sem("rows_in")
        wts_in = sem("wts_in")
        agg_zeroed = sem("agg_zeroed")
        dchain = sem("dchain")
        achain = sem("achain")
        pchain = sem("pchain")
        lasts_ready = sem("lasts_ready")
        lasts_turned = sem("lasts_turned")
        open_scanned = sem("open_scanned")
        open_turned = sem("open_turned")
        len_ready = sem("len_ready")
        rdeg_ready = sem("rdeg_ready")
        rows_ready = sem("rows_ready")
        cols_turned = sem("cols_turned")
        cols_ready = sem("cols_ready")
        seg_out = sem("seg_out")
        onehot = sem("onehot")
        counted = sem("counted")
        cnt_ready = sem("cnt_ready")
        cnt_turned = sem("cnt_turned")
        tab_inv = sem("tab_inv")
        tab_ready = sem("tab_ready")
        tab_out = sem("tab_out")

        ea_in = sems("ea_in", 2)
        segq_in = sems("segq_in", 2)
        xs_in = sems("xs_in", 2)
        ds_in = sems("ds_in", 2)
        scattered = sems("scattered", 2)
        gidx_ready = sem("gidx_ready")
        sidx_ready = sem("sidx_ready")
        eaT_done = sem("eaT_done")
        eaT_ready = sem("eaT_ready")
        h_done = sem("h_done")
        h_ready = sem("h_ready")
        m_done = sem("m_done")
        msg_ready = sem("msg_ready")
        masks_ready = sem("masks_ready")
        tile_summed = sem("tile_summed")
        sums_ready = sem("sums_ready")
        scaled_ready = sem("scaled_ready")

        xn_in = sems("xn_in", XR)
        ag_in = sems("ag_in", XR)
        out_sent = sems("out_sent", 2)
        xe_ready = sem("xe_ready")
        comb_ready = sem("comb_ready")
        cT_done = sem("cT_done")
        cT_ready = sem("cT_ready")
        hn_done = sem("hn_done")
        hn_ready = sem("hn_ready")
        o_done = sem("o_done")
        res_ready = sem("res_ready")
        rw_ready = sem("rw_ready")
        ssq_ready = sem("ssq_ready")
        rin_ready = sem("rin_ready")
        rrt_ready = sem("rrt_ready")
        y_ready = sem("y_ready")
        mean_ready = sem("mean_ready")
        var_ready = sem("var_ready")
        vin_ready = sem("vin_ready")
        vrt_ready = sem("vrt_ready")
        fin_ready = sem("fin_ready")
        sp_passed = sem("sp_passed")
        pool_passed = sem("pool_passed")
        dve_passed = sem("dve_passed")
        pe_passed = sem("pe_passed")
        rin_sum = sem("rin_sum")
        vin_sum = sem("vin_sum")

        block = ctx.enter_context(nc.Block())

        def at(n):
            return n.value() if isinstance(n, Count) else n

        def need(eng, s, value):
            if not (isinstance(value, int) and value <= 0):
                eng.wait_ge(s, at(value))

        def apart(eng, passed):
            eng.sem_inc(passed, 1)

        def run(eng, total, unroll, step, tail=0, head=1, peel=0):
            rounds = total // unroll - peel
            for n in range(head * unroll):
                step(n, n % unroll)
            with eng.Fori(head, rounds) as i:
                for u in range(unroll):
                    step(Count(i, unroll, u), u)
            for n in range(rounds * unroll, total + tail):
                step(n, n % unroll)

        def live(n, total):
            return not isinstance(n, int) or 0 <= n < total

        def block_loads(B):
            return (B // XR + 1 + (isinstance(B, int) and B == BLOCKS - 1)) * 16

        ZERO_COLS = 2 * BN
        ZERO_DMAS = -(-NPP // ZERO_COLS) + 1

        ROW_DMAS = 13

        def index_rows(eng, tile, a, off):
            lo = 1 if off < 0 else 0
            n = 0
            if off < 0:
                eng.dma_start(tile[0:1, 0, 1:P], a[0:P - 1].rearrange("(o c) -> o c", o=1)).then_inc(rows_in, 16)
                eng.dma_start(tile[1:P, 0, :], a[P + off:P * P + off].rearrange("(p c) -> p c", c=P)).then_inc(rows_in, 16)
                n += 2
            span = P * P * (CH - 1)
            eng.dma_start(tile[:, lo:CH - 1, :],
                          a[lo * P * P + off:span + off].rearrange("(k p c) -> p k c", p=P, c=P)).then_inc(rows_in, 16)
            more = FULL - P * (CH - 1)
            eng.dma_start(tile[0:more, CH - 1, :],
                          a[span + off:FULL * P + off].rearrange("(p c) -> p c", c=P)).then_inc(rows_in, 16)
            eng.dma_start(tile[more:more + 1, CH - 1, 0:REST - off],
                          a[FULL * P + off:E].rearrange("(o c) -> o c", o=1)).then_inc(rows_in, 16)
            return n + 3

        x_main = x[0:NPP * P, :].rearrange("(p i) d -> p i d", p=P)
        ag_main = agg_d[0:NPP * P, :].rearrange("(p i) d -> p i d", p=P)
        out_main = out[0:NPP * P, :].rearrange("(p i) d -> p i d", p=P)

        @block.sync
        def _(sp):
            sp.wait_ge(pads_set, 4)
            sent = 0
            for tile, a, off in ((dst_r, dst, 0), (nxt_r, dst, 1), (prv_r, dst, -1), (src_r, src, 0)):
                sent += index_rows(sp, tile, a, off)
            assert 16 * sent == 16 * (ROW_DMAS + 1)
            for o, i in ((w1e[:, :], W1e), (w2e[:, :], W2e), (w1n[:, :], W1n), (w2n[:, :], W2n),
                         (b1e_c[:, :], b1e.rearrange("(p o) -> p o", o=1)),
                         (b1n_c[:, :], b1n.rearrange("(p o) -> p o", o=1)),
                         (rms_b[:, :], rms_w.rearrange("(o d) -> o d", o=1).partition_broadcast(P)),
                         (eps1[:, :], gin_eps.rearrange("(o d) -> o d", o=1).partition_broadcast(P)),
                         (bias_f[:, 0, :], b2e.rearrange("(o d) -> o d", o=1).partition_broadcast(P)),
                         (bias_f[:, 1, :], b2n.rearrange("(o d) -> o d", o=1).partition_broadcast(P))):
                sp.dma_start(o, i).then_inc(wts_in, 16)
            sp.wait_ge(rows_ready, 1)
            sp.dma_start(seg_d[:].rearrange("(k p c) -> p k c", p=P, c=P), seg_b[:, :, :]).then_inc(seg_out, 16)
            sp.wait_ge(seg_out, 16)

            def edge_loads(b, u):
                s = u % 2
                need(sp, eaT_done, b - 1)
                apart(sp, sp_passed)
                if isinstance(b, int) and b * W + W > E:
                    whole = FULL - b * TB
                    sp.dma_start(ea[:, s, 0:whole, :],
                                 edge_attr[b * W:FULL * P, :].rearrange("(j p) d -> p j d", p=P)).then_inc(ea_in[s], 16)
                    sp.dma_start(ea[0:REST, s, whole, :], edge_attr[FULL * P:E, :]).then_inc(ea_in[s], 16)
                else:
                    sp.dma_start(ea[:, s, :, :],
                                 edge_attr[bass.ds(at(b * W), W), :].rearrange("(j p) d -> p j d", p=P)).then_inc(ea_in[s], 16)
                need(sp, masks_ready, b - 1)
                apart(sp, sp_passed)
                sp.dma_start(segq[:, s, :],
                             seg_d[bass.ds(at(b * W), W)].rearrange("(o c) -> o c", o=1).partition_broadcast(P)
                             ).then_inc(segq_in[s], 16)

            run(sp, BATCHES, 2, edge_loads, peel=1)

            for s in range(2):
                sp.wait_ge(scattered[s], 16 * TB * (BATCHES // 2))

            def node_block(B, u):
                s = u % XR
                if live(B, BLOCKS):
                    need(sp, y_ready, (B - XR + 1) * SPB)
                    need(sp, comb_ready, (B - XR + 1) * SPB)
                    for t, d, view, s_in in ((xn, x, x_main, xn_in), (ag, agg_d, ag_main, ag_in)):
                        if isinstance(B, int) and B == BLOCKS - 1:
                            sp.dma_start(t[:, s, 0:LASTC, :], view[:, B * BN:NPP, :]).then_inc(s_in[s], 16)
                            sp.dma_start(t[0:NREM, s, LASTC, :], d[NPP * P:N, :]).then_inc(s_in[s], 16)
                        else:
                            sp.dma_start(t[:, s, :, :], view[:, bass.ds(at(B * BN), BN), :]).then_inc(s_in[s], 16)
                C, o = B - XR, (u - XR) % 2
                if live(C, BLOCKS):
                    need(sp, fin_ready, (C + 1) * SPB)
                    if isinstance(C, int) and C == BLOCKS - 1:
                        sp.dma_start(out_main[:, C * BN:NPP, :], on[:, o, 0:LASTC, :]).then_inc(out_sent[o], 16)
                        sp.dma_start(out[NPP * P:N, :], on[0:NREM, o, LASTC, :]).then_inc(out_sent[o], 16)
                    else:
                        sp.dma_start(out_main[:, bass.ds(at(C * BN), BN), :], on[:, o, :, :]).then_inc(out_sent[o], 16)

            run(sp, BLOCKS, XR, node_block, tail=XR)
            for o in range(2):
                blocks = len(range(o, BLOCKS, 2))
                sp.wait_ge(out_sent[o], 16 * (blocks + int((BLOCKS - 1) % 2 == o)))

        @block.gpsimd
        def _(pool):
            for t, v in ((dst_r, NO_NODE), (nxt_r, NO_NODE), (prv_r, NO_NODE), (src_r, 0)):
                pool.memset(t[:, :, :], v).then_inc(pads_set, 1)
            pool.memset(on[:, :, :, :], 0.0).then_inc(zero_set, 1)
            pool.memset(ident[:, :], 0.0).then_inc(pchain, 1)
            pool.wait_ge(pchain, 1)
            pool.affine_select(out=ident[:, :], in_=ident[:, :], compare_op=ALU.not_equal, fill=1.0, base=0,
                               pattern=[[-1, P]], channel_multiplier=1).then_inc(ident_s, 1)
            pool.iota(iota_i[:, :], pattern=[[1, HIGH]], base=0, channel_multiplier=0).then_inc(consts, 1)
            pool.iota(gidx_i[:, :, :], pattern=[[P * P, CH], [1, P]], base=0, channel_multiplier=P).then_inc(consts, 1)
            pool.memset(ones[:, :], 1.0).then_inc(consts, 1)
            pool.memset(ones_b[:, :], 1.0).then_inc(consts, 1)
            pool.memset(cnt[:, :], 0.0).then_inc(consts, 1)
            pool.memset(ea[:, :, :, :], 0.0).then_inc(consts, 1)

            def gathers(b, u):
                s = u % 2
                if live(b, BATCHES):
                    pool.wait_ge(gidx_ready, at(b + 1))
                    need(pool, msg_ready, b - 1)
                    apart(pool, pool_passed)
                    for j in range(TB):
                        pool.indirect_dma_start(out=xs[:, s, j, :], out_offset=None, in_=x,
                                                in_offset=bass.IndirectOffsetOnAxis(ap=gat_i[:, s, j:j + 1], axis=0)
                                                ).then_inc(xs_in[s], 16)
                    if isinstance(b, int) and b == 0:
                        pool.wait_ge(tab_out, 16)
                    need(pool, masks_ready, b - 1)
                    apart(pool, pool_passed)
                    for j in range(TB):
                        pool.indirect_dma_start(out=ds[:, s, j:j + 1], out_offset=None, in_=tab_rows,
                                                in_offset=bass.IndirectOffsetOnAxis(ap=gat_i[:, s, j:j + 1], axis=0)
                                                ).then_inc(ds_in[s], 16)
                c = b - 2
                if live(c, BATCHES):
                    if isinstance(c, int) and c == 0:
                        pool.wait_ge(agg_zeroed, ZERO_DMAS * 16)
                    pool.wait_ge(sidx_ready, at(c + 1))
                    for j in range(TB):
                        pool.wait_ge(scaled_ready, at(c * TB + j + 1))
                        apart(pool, pool_passed)
                        pool.indirect_dma_start(out=agg_rows,
                                                out_offset=bass.IndirectOffsetOnAxis(ap=sca_i[:, s, j:j + 1], axis=0),
                                                in_=scaled[:, s, j, :], in_offset=None,
                                                bounds_check=N - 1, oob_is_err=False).then_inc(scattered[s], 16)

            run(pool, BATCHES, 2, gathers, tail=2)

            def node_step(n, u):
                m, s = n - 5, (u - 5) % 4
                if live(m, STEPS):
                    pool.wait_ge(res_ready, at(m + 1))
                    need(pool, y_ready, m - 3)
                    pool.tensor_tensor(rw[:, s, :, :], res[:, s % 2, :, :],
                                       rms_b[:, :].unsqueeze(1).to_broadcast([P, TB, D]), ALU.mult).then_inc(rw_ready, 1)
                m, s = n - 1, (u - 1) % 2
                if live(m, STEPS):
                    B, xsl, h = m // SPB, ((u - 1) // SPB) % XR, ((u - 1) % SPB) * TB
                    pool.wait_ge(ag_in[xsl], at(block_loads(B)))
                    pool.wait_ge(xe_ready, at(m + 1))
                    need(pool, cT_done, m - 1)
                    pool.tensor_tensor(comb[:, s, :, :], xe[:, s, :, :], ag[:, xsl, h:h + TB, :],
                                       ALU.add).then_inc(comb_ready, 1)

            run(pool, STEPS, SPB * XR, node_step, tail=5)

        @block.scalar
        def _(act):
            act.wait_ge(rows_in, 16 * (ROW_DMAS + 1))
            act.wait_ge(zero_set, 1)
            for c in range(0, NPP, ZERO_COLS):
                w = min(ZERO_COLS, NPP - c)
                act.dma_start(ag_main[:, c:c + w, :],
                              on.rearrange("p o i d -> p (o i) d")[:, 0:w, :]).then_inc(agg_zeroed, 16)
            act.dma_start(agg_d[NPP * P:N, :], on[0:NREM, 0, 0, :]).then_inc(agg_zeroed, 16)

            act.wait_ge(len_ready, 1)
            act.activation(rows[RDEG][:, :, :], rows[RDEG][:, :, :], ACT.Sqrt).then_inc(rdeg_ready, 1)
            for k in range(6):
                act.wait_ge(cols_turned, k + 1)
                act.activation(cols[k][:, :], ps[4 + k % 2][:, :], ACT.Copy).then_inc(cols_ready, 1)
            act.wait_ge(tab_inv, 1)
            act.activation(tab[:, :], tab[:, :], ACT.Sqrt).then_inc(tab_ready, 1)
            act.wait_ge(tab_ready, 1)
            act.dma_start(tab_d[:, :].rearrange("(c p l) o -> p c (l o)", p=P, l=P),
                          tab[:, :].rearrange("p (c l) -> p c l", l=P)).then_inc(tab_out, 16)

            def tile_out(b, u, j):
                s = u % 2
                t = b * TB + j
                act.wait_ge(tile_summed, at(t + 1))
                act.activation(sums[:, j % 2, :], ps[6 + j % 2][:, 0:D], ACT.Copy).then_inc(sums_ready, 1)
                if j == 0:
                    act.wait_ge(sidx_ready, at(b + 1))
                    need(act, scattered[s], b // 2 * 16 * TB)
                act.activation(scaled[:, s, j, :], ps[6 + j % 2][:, 0:D], ACT.Copy,
                               scale=rdg[:, s, j:j + 1]).then_inc(scaled_ready, 1)

            def edge_step(b, u):
                s = u % 2
                if live(b, BATCHES):
                    act.wait_ge(eaT_done, at(b + 1))
                    need(act, h_done, b - 1)
                    act.activation(eaT[:, s, :], ps[2][0:ED, :], ACT.Copy).then_inc(eaT_ready, 1)
                if live(b - 1, BATCHES):
                    tile_out(b - 1, u - 1, 0)
                if live(b, BATCHES):
                    act.wait_ge(h_done, at(b + 1))
                    need(act, m_done, b - 1)
                    act.activation(he[:, s, :], ps[3][:, :], ACT.Relu, bias=b1e_c[:, 0:1]).then_inc(h_ready, 1)
                if live(b - 1, BATCHES):
                    for j in range(1, TB):
                        tile_out(b - 1, u - 1, j)

            act.wait_ge(wts_in, 160)
            run(act, BATCHES, 2, edge_step, tail=1)

            def node_step(n, u):
                m, s = n - 6, (u - 6) % 2
                if live(m, STEPS):
                    act.wait_ge(rin_ready, at(m + 1))
                    need(act, y_ready, m - 1)
                    act.activation(rrt[:, s, :], rin[:, s, :], ACT.Sqrt).then_inc(rrt_ready, 1)
                m, s = n - 9, (u - 9) % 2
                if live(m, STEPS):
                    act.wait_ge(vin_ready, at(m + 1))
                    need(act, fin_ready, m - 1)
                    act.activation(vrt[:, s, :], vin[:, s, :], ACT.Sqrt).then_inc(vrt_ready, 1)
                m, s = n - 5, (u - 5) % 2
                if live(m, STEPS):
                    act.wait_ge(res_ready, at(m + 1))
                    need(act, rin_ready, m - 1)
                    for j in range(TB):
                        last = act.activation(squares[:, s, j, :], res[:, s, j, :], ACT.Square,
                                              accum_out=ssq[:, s, j:j + 1])
                    last.then_inc(ssq_ready, 1)
                m, s = n - 2, (u - 2) % 2
                if live(m, STEPS):
                    act.wait_ge(cT_done, at(m + 1))
                    need(act, hn_done, m - 1)
                    act.activation(cT[:, s, :], ps[s][:, :], ACT.Copy).then_inc(cT_ready, 1)
                s = u % 2
                if live(n, STEPS):
                    B, xsl, h = n // SPB, (u // SPB) % XR, (u % SPB) * TB
                    act.wait_ge(xn_in[xsl], at(block_loads(B)))
                    need(act, comb_ready, n - 1)
                    act.activation(xe[:, s, :, :], xn[:, xsl, h:h + TB, :], ACT.Copy,
                                   scale=eps1[:, 0:1]).then_inc(xe_ready, 1)
                m, s = n - 8, (u - 8) % 4
                if live(m, STEPS):
                    act.wait_ge(mean_ready, at(m + 1))
                    need(act, vin_ready, m - 1)
                    for j in range(TB):
                        last = act.activation(deviations[:, s % 2, j, :], yn[:, s, j, :], ACT.Square,
                                              bias=neg_mean[:, s, j:j + 1], accum_out=var_sum[:, s % 2, j:j + 1])
                    last.then_inc(var_ready, 1)
                m, s = n - 3, (u - 3) % 2
                if live(m, STEPS):
                    act.wait_ge(hn_done, at(m + 1))
                    need(act, o_done, m - 1)
                    act.activation(hn[:, s, :], ps[2 + s][:, :], ACT.Relu, bias=b1n_c[:, 0:1]).then_inc(hn_ready, 1)

            run(act, STEPS, SPB * XR, node_step, tail=9)

        @block.vector
        def _(dve):
            done = [0]

            def link(ins):
                done[0] += 1
                ins.then_inc(dchain, 1)
                dve.wait_ge(dchain, done[0])

            dve.wait_ge(consts, 6)
            dve.tensor_copy(iota_h[:, :], iota_i[:, :])
            link(dve.tensor_copy(gidx[:, :, :], gidx_i[:, :, :]))
            dve.wait_ge(rows_in, 16 * (ROW_DMAS + 1))
            dve.tensor_copy(dst_f[:, :, :], dst_r[:, :, :])
            dve.tensor_copy(nxt_f[:, :, :], nxt_r[:, :, :])
            dve.tensor_scalar(hi_r[:, :, :], dst_r[:, :, :], 7, None, ALU.arith_shift_right)
            dve.tensor_scalar(lo_r[:, :, :], dst_r[:, :, :], P - 1, None, ALU.bitwise_and)
            dve.tensor_copy(rows[SRC][:, :, :], src_r[:, :, :])
            link(dve.tensor_copy(prv_f[:, :, :], prv_r[:, :, :]))
            dve.tensor_copy(rows[HI][:, :, :], hi_r[:, :, :])
            dve.tensor_copy(rows[LO][:, :, :], lo_r[:, :, :])
            dve.tensor_tensor(nxt_f[:, :, :], dst_f[:, :, :], nxt_f[:, :, :], ALU.is_equal)
            link(dve.tensor_tensor(new_f[:, :, :], dst_f[:, :, :], prv_f[:, :, :], ALU.not_equal))
            dve.scalar_tensor_tensor(rows[SCAT][:, :, :], nxt_f[:, :, :], SKIP, dst_f[:, :, :], ALU.mult, ALU.add)
            link(dve.scalar_tensor_tensor(fst_f[:, :, :], gidx[:, :, :], 1.0, new_f[:, :, :], ALU.add, ALU.mult))
            for k in range(CH):
                dve.tensor_tensor_scan(rows[SEG][:, k, :], ones[:, :], new_f[:, k, :], 0.0, ALU.mult, ALU.add)
                last = dve.tensor_tensor_scan(prv_f[:, k, :], ones[:, :], fst_f[:, k, :], 0.0, ALU.mult, ALU.max)
            link(last)
            last = dve.tensor_copy(seg_b[:, :, :], rows[SEG][:, :, :])
            dve.tensor_copy(open_col[:, :], prv_f[:, :, P - 1]).then_inc(lasts_ready, 1)
            link(last)
            dve.memset(open_row[:, 0:1], 0.0)
            dve.wait_ge(lasts_turned, 1)
            link(dve.tensor_copy(open_in[:, :], ps[4][0:1, :]))
            link(dve.tensor_tensor_scan(open_row[:, 1:CH * P + 1], open_in[:, :], open_in[:, :], 0.0,
                                        ALU.max, ALU.max))
            dve.sem_inc(open_scanned, 1)
            dve.wait_ge(open_turned, 1)
            link(dve.tensor_copy(open_col[:, :], ps[5][:, 0:CH]))
            for k in range(CH):
                last = dve.tensor_scalar(fst_f[:, k, :], prv_f[:, k, :], open_col[:, k:k + 1], None, ALU.max)
            link(last)
            link(dve.scalar_tensor_tensor(new_f[:, :, :], fst_f[:, :, :], -1.0, gidx[:, :, :], ALU.mult, ALU.add))
            link(dve.tensor_scalar(new_f[:, :, :], new_f[:, :, :], 2.0, None, ALU.add))
            dve.reciprocal(rows[RDEG][:, :, :], new_f[:, :, :]).then_inc(len_ready, 1)
            dve.sem_inc(rows_ready, 1)

            dve.wait_ge(wts_in, 160)
            link(dve.tensor_scalar(eps1[:, :], eps1[:, :], 1.0, None, ALU.add))
            dve.wait_ge(ident_s, 1)
            for k in range(3):
                link(dve.tensor_copy(bias_p[:, :, :], bias_f[:, :, :]))
                link(dve.tensor_copy(bias_r[:, :, :], bias_p[:, :, :]))
                if k == 0:
                    link(dve.tensor_scalar(bias_s[:, :, :], bias_r[:, :, :], ident[:, k:k + 1], None, ALU.mult))
                else:
                    link(dve.scalar_tensor_tensor(bias_s[:, :, :], bias_r[:, :, :], ident[:, k:k + 1],
                                                  bias_s[:, :, :], ALU.mult, ALU.add))
                link(dve.tensor_tensor(bias_f[:, :, :], bias_f[:, :, :], bias_r[:, :, :], ALU.subtract))
            for j in range(TB):
                last = dve.tensor_copy(bias[:, :, j, :], bias_s[:, :, :])
            link(last)

            dve.wait_ge(cols_ready, 6)

            def count_step(b, u):
                s = u % 2
                need(dve, counted, b - 1)
                for j in range(TB):
                    dve.tensor_scalar(oh_hi[:, s, j, :], iota_h[:, :], cols[HI][:, bass.ds(at(b * TB + j), 1)], None,
                                      ALU.is_equal)
                    dve.tensor_scalar(oh_lo[:, s, j, :], iota_h[:, 0:P], cols[LO][:, bass.ds(at(b * TB + j), 1)], None,
                                      ALU.is_equal).then_inc(onehot, 1)

            run(dve, BATCHES, 2, count_step)
            dve.wait_ge(counted, BATCHES)
            dve.tensor_copy(cnt[:, 0:512], ps[0][:, :])
            dve.tensor_copy(cnt[:, 512:HIGH], ps[1][:, 0:HIGH - 512]).then_inc(cnt_ready, 1)
            dve.wait_ge(cnt_turned, 1)
            dve.tensor_scalar(tab[:, 0:512], ps[4][:, :], 1.0, None, ALU.max)
            link(dve.tensor_scalar(tab[:, 512:HCH * P], ps[5][:, 0:HCH * P - 512], 1.0, None, ALU.max))
            dve.reciprocal(tab[:, :], tab[:, :]).then_inc(tab_inv, 1)

            def gather_indices(b, u):
                dve.tensor_copy(gat_i[:, u % 2, :], cols[SRC][:, bass.ds(at(b * TB), TB)]).then_inc(gidx_ready, 1)

            def edge_step(b, u):
                s = u % 2
                if live(b + 1, BATCHES):
                    need(dve, xs_in[1 - s], (b + 1) // 2 * 16 * TB)
                    need(dve, ds_in[1 - s], (b + 1) // 2 * 16 * TB)
                    gather_indices(b + 1, u + 1)
                need(dve, scattered[s], b // 2 * 16 * TB)
                dve.tensor_copy(sca_i[:, s, :], cols[SCAT][:, bass.ds(at(b * TB), TB)])
                dve.tensor_copy(rdg[:, s, :], cols[RDEG][:, bass.ds(at(b * TB), TB)]).then_inc(sidx_ready, 1)
                dve.wait_ge(segq_in[s], at((b // 2 + 1) * 16))
                need(dve, tile_summed, (b - 1) * TB)
                dve.tensor_scalar(carry[:, s, :, :].rearrange("p j c -> p (j c)"), segq[:, s, :], 0.0,
                                  ident[:, P - 1:P], ALU.is_equal, ALU.mult)
                dve.wait_ge(ds_in[s], at((b // 2 + 1) * 16 * TB))
                for j in range(TB):
                    last = dve.tensor_scalar(same[:, s, j, :], segq[:, s, j * P:(j + 1) * P],
                                             cols[SEG][:, bass.ds(at(b * TB + j), 1)], ds[:, s, j:j + 1],
                                             ALU.is_equal, ALU.mult)
                last.then_inc(masks_ready, 1)
                dve.wait_ge(xs_in[s], at((b // 2 + 1) * 16 * TB))
                dve.wait_ge(m_done, at(b + 1))
                dve.tensor_tensor(msg[:, s, :, :].rearrange("p j d -> p (j d)"), ps[4 + s][:, :],
                                  xs[:, s, :, :].rearrange("p j d -> p (j d)"), ALU.add).then_inc(msg_ready, 1)

            gather_indices(0, 0)
            run(dve, BATCHES, 2, edge_step, peel=1)

            def node_step(n, u):
                m, s = n - 7, (u - 7) % 4
                if live(m, STEPS):
                    xsl, h = ((u - 7) // SPB) % XR, ((u - 7) % SPB) * TB
                    dve.wait_ge(rrt_ready, at(m + 1))
                    dve.wait_ge(rw_ready, at(m + 1))
                    need(dve, fin_ready, m - 3)
                    for j in range(TB):
                        last = dve.scalar_tensor_tensor(yn[:, s, j, :], rw[:, s, j, :], rrt[:, s % 2, j:j + 1],
                                                        xn[:, xsl, h + j, :], ALU.mult, ALU.add,
                                                        accum_out=ysum[:, s % 2, j:j + 1])
                    last.then_inc(y_ready, 1)
                m, s = n - 4, (u - 4) % 2
                if live(m, STEPS):
                    xsl, h = ((u - 4) // SPB) % XR, ((u - 4) % SPB) * TB
                    dve.wait_ge(o_done, at(m + 1))
                    need(dve, ssq_ready, m - 1)
                    need(dve, rw_ready, m - 1)
                    dve.tensor_tensor(res[:, s, :, :].rearrange("p j d -> p (j d)"), ps[4 + s][:, :],
                                      xn[:, xsl, h:h + TB, :].rearrange("p j d -> p (j d)"),
                                      ALU.add).then_inc(res_ready, 1)
                m, s = n - 7, (u - 7) % 4
                if live(m, STEPS):
                    dve.wait_ge(y_ready, at(m + 1))
                    dve.tensor_scalar(neg_mean[:, s, :], ysum[:, s % 2, :], -1.0 / D, None,
                                      ALU.mult).then_inc(mean_ready, 1)
                m, s = n - 10, (u - 10) % 4
                if live(m, STEPS):
                    B, o, h = m // SPB, ((u - 10) // SPB) % 2, ((u - 10) % SPB) * TB
                    dve.wait_ge(vrt_ready, at(m + 1))
                    if (u - 10) % SPB == 0:
                        need(dve, out_sent[o], B // 2 * 16)
                    for j in range(TB):
                        last = dve.tensor_scalar(on[:, o, h + j, :], yn[:, s, j, :], neg_mean[:, s, j:j + 1],
                                                 vrt[:, s % 2, j:j + 1], ALU.add, ALU.mult)
                    last.then_inc(fin_ready, 1)
                m, s = n - 5, (u - 5) % 2
                if live(m, STEPS):
                    dve.wait_ge(ssq_ready, at(m + 1))
                    need(dve, rrt_ready, m - 1)
                    dve.tensor_scalar(rin[:, s, :], ssq[:, s, :], 1.0 / D, RMS_EPS, ALU.mult, ALU.add
                                      ).then_inc(rin_sum, 1)
                    dve.wait_ge(rin_sum, at(m + 1))
                    dve.reciprocal(rin[:, s, :], rin[:, s, :]).then_inc(rin_ready, 1)
                m, s = n - 8, (u - 8) % 2
                if live(m, STEPS):
                    dve.wait_ge(var_ready, at(m + 1))
                    need(dve, vrt_ready, m - 1)
                    dve.tensor_scalar(vin[:, s, :], var_sum[:, s, :], 1.0 / D, LN_EPS, ALU.mult, ALU.add
                                      ).then_inc(vin_sum, 1)
                    dve.wait_ge(vin_sum, at(m + 1))
                    dve.reciprocal(vin[:, s, :], vin[:, s, :]).then_inc(vin_ready, 1)

            run(dve, STEPS, SPB * XR, node_step, tail=10)

        @block.tensor
        def _(pe):
            pe.wait_ge(ident_s, 1)
            pe.wait_ge(consts, 6)
            pe.wait_ge(lasts_ready, 1)
            for k in range(CH):
                last = pe.transpose(ps[4][0:1, k * P:(k + 1) * P], open_col[:, k:k + 1], ident[:, :])
            last.then_inc(lasts_turned, 1)
            pe.wait_ge(open_scanned, 1)
            for k in range(CH):
                last = pe.transpose(ps[5][:, k:k + 1], open_row[0:1, k * P:(k + 1) * P], ident[0:1, 0:1])
            last.then_inc(open_turned, 1)
            pe.wait_ge(rows_ready, 1)
            pe.wait_ge(rdeg_ready, 1)
            for k in range(6):
                need(pe, cols_ready, k - 1)
                for c in range(CH):
                    last = pe.transpose(ps[4 + k % 2][:, c * P:(c + 1) * P], rows[k][:, c, :], ident[:, :])
                last.then_inc(cols_turned, 1)

            def count_step(b, u):
                s = u % 2
                for j in range(TB):
                    pe.wait_ge(onehot, at(b * TB + j + 1))
                    first = isinstance(b, int) and b == 0 and j == 0
                    end = isinstance(b, int) and b == BATCHES - 1 and j == TB - 1
                    pe.matmul(ps[0][:, :], oh_lo[:, s, j, :], oh_hi[:, s, j, 0:512], start=first, stop=end)
                    last = pe.matmul(ps[1][:, 0:HIGH - 512], oh_lo[:, s, j, :], oh_hi[:, s, j, 512:HIGH],
                                     start=first, stop=end)
                last.then_inc(counted, 1)

            run(pe, BATCHES, 2, count_step, peel=1)
            pe.wait_ge(cnt_ready, 1)
            pe.wait_ge(cols_ready, 6)
            for c in range(HCH):
                last = pe.transpose(ps[4 + c // 4][:, (c % 4) * P:(c % 4 + 1) * P], cnt[:, c * P:(c + 1) * P],
                                    ident[:, :])
            last.then_inc(cnt_turned, 1)

            pe.wait_ge(wts_in, 160)
            pe.wait_ge(tab_inv, 1)

            def tile_sum(b, u, j):
                s = u % 2
                t = b * TB + j
                if j == 0:
                    pe.wait_ge(msg_ready, at(b + 1))
                    pe.wait_ge(masks_ready, at(b + 1))
                need(pe, scaled_ready, t - 1)
                first = isinstance(t, int) and t == 0
                last = pe.matmul(ps[6 + j % 2][:, 0:D], same[:, s, j, :], msg[:, s, j, :], start=True, stop=first)
                if not first:
                    pe.wait_ge(sums_ready, at(t))
                    last = pe.matmul(ps[6 + j % 2][:, 0:D], carry[:, s, j, :], sums[:, (j - 1) % 2, :],
                                     start=False, stop=True)
                last.then_inc(tile_summed, 1)

            def edge_step(b, u):
                s = u % 2
                if live(b, BATCHES):
                    loads = (b // 2 + 1) * 16 + (16 if isinstance(b, int) and b * W + W > E else 0)
                    pe.wait_ge(ea_in[s], at(loads))
                    need(pe, eaT_ready, b)
                    apart(pe, pe_passed)
                    for j in range(TB):
                        last = pe.transpose(ps[2][0:ED, j * P:(j + 1) * P], ea[:, s, j, :], ident[:, :])
                    last.then_inc(eaT_done, 1)
                if live(b - 1, BATCHES):
                    tile_sum(b - 1, u - 1, 0)
                if live(b, BATCHES):
                    pe.wait_ge(eaT_ready, at(b + 1))
                    need(pe, h_ready, b)
                    pe.matmul(ps[3][:, :], w1e[:, :], eaT[:, s, :], start=True, stop=True).then_inc(h_done, 1)
                if live(b - 1, BATCHES):
                    tile_sum(b - 1, u - 1, 1)
                if live(b, BATCHES):
                    need(pe, msg_ready, b - 1)
                    pe.matmul(ps[4 + s][:, :], ones_b[:, :], bias[:, 0, :, :].rearrange("p j d -> p (j d)"),
                              start=True, stop=False)
                    pe.wait_ge(h_ready, at(b + 1))
                    for j in range(TB):
                        last = pe.matmul(ps[4 + s][:, j * P:(j + 1) * P], he[:, s, j * P:(j + 1) * P], w2e[:, :],
                                         start=False, stop=j == TB - 1)
                    last.then_inc(m_done, 1)
                if live(b - 1, BATCHES):
                    tile_sum(b - 1, u - 1, 2)
                    tile_sum(b - 1, u - 1, 3)

            run(pe, BATCHES, 2, edge_step, tail=1, peel=1)

            def node_step(n, u):
                m, s = n - 4, (u - 4) % 2
                if live(m, STEPS):
                    need(pe, res_ready, m - 1)
                    pe.matmul(ps[4 + s][:, :], ones_b[:, :], bias[:, 1, :, :].rearrange("p j d -> p (j d)"),
                              start=True, stop=False)
                    pe.wait_ge(hn_ready, at(m + 1))
                    for j in range(TB):
                        last = pe.matmul(ps[4 + s][:, j * P:(j + 1) * P], hn[:, s, j * P:(j + 1) * P], w2n[:, :],
                                         start=False, stop=j == TB - 1)
                    last.then_inc(o_done, 1)
                m, s = n - 2, (u - 2) % 2
                if live(m, STEPS):
                    pe.wait_ge(comb_ready, at(m + 1))
                    need(pe, cT_ready, m - 1)
                    for j in range(TB):
                        last = pe.transpose(ps[s][:, j * P:(j + 1) * P], comb[:, s, j, :], ident[:, :])
                    last.then_inc(cT_done, 1)
                m, s = n - 3, (u - 3) % 2
                if live(m, STEPS):
                    pe.wait_ge(cT_ready, at(m + 1))
                    need(pe, hn_ready, m - 1)
                    pe.matmul(ps[2 + s][:, :], w1n[:, :], cT[:, s, :], start=True, stop=True).then_inc(hn_done, 1)

            run(pe, STEPS, SPB * XR, node_step, tail=4)


_INS = ['x', 'src', 'dst', 'edge_attr_64', 'L0_gnn_W1n', 'L0_gnn_b1n', 'L0_gnn_W2n', 'L0_gnn_b2n', 'L0_gnn_W1e',
        'L0_gnn_b1e', 'L0_gnn_W2e', 'L0_gnn_b2e', 'L0_gnn_gin_eps', 'L0_gnn_rms_w']


def kernel(**inputs):
    import numpy as _np
    import concourse.bacc as _bacc
    from concourse import mybir as _mybir
    from concourse.bass_utils import run_bass_kernel_spmd as _run

    nc = _bacc.Bacc("TRN2", target_bir_lowering=False, num_devices=1)
    arrays, args = {}, []
    for name in _INS:
        a = _np.asarray(inputs[name])
        a = _np.ascontiguousarray(a.reshape(a.shape or (1,)))
        arrays[f"in_{name}"] = a
        args.append(nc.dram_tensor(f"in_{name}", a.shape, _mybir.dt.from_np(a.dtype), kind="ExternalInput").ap())
    out = nc.dram_tensor("out_0", arrays["in_x"].shape, _mybir.dt.float32, kind="ExternalOutput").ap()
    build(nc, *args, out)
    r = _run(nc, [arrays], core_ids=[0])
    return r.results[0]["out_0"]
```

```python
import concourse.bass as bass
from concourse import mybir
from contextlib import ExitStack


class Count:

    def __init__(self, i, per, base, first=1):
        self.i, self.per, self.base, self.first = i, per, base, first

    def __add__(self, k):
        return Count(self.i, self.per, self.base + k, self.first)

    def __sub__(self, k):
        return Count(self.i, self.per, self.base - k, self.first)

    def __mul__(self, k):
        return Count(self.i, self.per * k, self.base * k, self.first)

    def __floordiv__(self, k):
        assert self.per % k == 0
        return Count(self.i, self.per // k, self.base // k, self.first)

    def value(self):
        return self.i * self.per + self.base if self.base >= 0 else self.i * self.per - -self.base


def build(nc, x, src, dst, edge_attr, W1n, b1n, W2n, b2n, W1e, b1e, W2e, b2e, gin_eps, rms_w, out):
    f32 = mybir.dt.float32
    bf16 = mybir.dt.bfloat16
    f16 = mybir.dt.float16
    i32 = mybir.dt.int32
    ALU = mybir.AluOpType
    ACT = mybir.ActivationFunctionType

    P = 128
    N, D = x.shape
    E, ED = edge_attr.shape
    RMS_EPS = 1.1920929e-07
    LN_EPS = 1e-05

    TB = 4
    W = TB * P
    TILES = -(-E // P)
    BATCHES = -(-TILES // TB)
    BATCHES += BATCHES % 2
    FULL = E // P
    REST = E - FULL * P
    CH = TB
    assert BATCHES * TB <= CH * P and FULL // P == CH - 1
    NO_NODE = 2 * N
    XS = 24
    SC = 8
    ROUND, ROUND_IN = 32, XS
    SPREAD = ROUND - 1
    ROUNDS = BATCHES // ROUND
    FIRST_IN = BATCHES - XS - (ROUNDS - 1) * ROUND_IN
    HQ = 4
    assert XS % SC == 0 and ROUND % SC == 0 and ROUND_IN <= FIRST_IN <= SPREAD and XS % HQ == 0
    SKIP = 1000000.0

    HIGH = -(-N // P)
    HIGH += HIGH % 2
    HCH = -(-HIGH // P)
    DIGIT = 2048
    assert E < 65504

    NPP = N // P
    NREM = N - NPP * P
    BN = 16
    SPB = BN // TB
    BLOCKS = -(-(NPP + 1) // BN)
    LASTC = NPP - (BLOCKS - 1) * BN
    assert 0 < LASTC < BN
    STEPS = SPB * BLOCKS
    XR, AR = 4, 2
    VAR_LAG = 4

    agg_d = nc.dram_tensor("agg_scratch", (N, D), f32)
    high_d = nc.dram_tensor("src_high_scratch", (CH * P * P,), f16)
    seg_d = nc.dram_tensor("segment_number_scratch", (CH * P * P,), bf16)
    agg_rows = agg_d[:, :]

    with ExitStack() as ctx:
        def sb(name, shape, dt=f32):
            return ctx.enter_context(nc.sbuf_tensor(name, shape, dt))

        def sem(name):
            return ctx.enter_context(nc.semaphore(name))

        def sems(name, n):
            return [sem(f"{name}{i}") for i in range(n)]

        ident = sb("ident", [P, P])
        iota_i = sb("iota_i", [P, HIGH], i32)
        iota_h = sb("iota_h", [P, HIGH], f16)
        gidx_i = sb("gidx_i", [P, CH, P], i32)
        gidx = sb("gidx", [P, CH, P])
        high_i = sb("high_i", [P, HCH], i32)
        high_no = sb("high_no", [P, HCH])
        ones = sb("ones", [P, P])
        ones_b = sb("ones_b", [P, P], bf16)
        xn = sb("xn", [P, XR, BN, D])
        on = sb("on", [P, 2, BN, D])
        w1e = sb("w1e", [ED, D])
        w2e = sb("w2e", [D, D])
        w1n = sb("w1n", [D, D])
        w2n = sb("w2n", [D, D])
        b1e_c = sb("b1e_c", [D, 1])
        b1n_c = sb("b1n_c", [D, 1])
        rms_b = sb("rms_b", [P, D])
        eps1 = sb("eps1", [P, 1])
        epsilons = sb("epsilons", [P, 2 * TB])
        bias_f = sb("bias_f", [P, 2, D])
        bias_r = sb("bias_r", [P, 2, D])
        bias_s = sb("bias_s", [P, 2, D])
        bias_m = sb("bias_m", [P, 2, D])
        bias_p = sb("bias_p", [P, 2, D], bf16)
        bias = sb("bias", [P, 2, TB, D], bf16)

        persistent, early = ctx, ctx.enter_context(ExitStack())

        def sb(name, shape, dt=f32):
            return early.enter_context(nc.sbuf_tensor(name, shape, dt))

        HI, STEP, SRC, SRC_LO, SCAT, SEG, LEN = range(7)
        COLS = 7
        cols = [sb(f"cols{k}", [P, CH * P]) for k in range(COLS)]
        high_b = sb("high_b", [P, CH, P], f16)
        seg_b = sb("seg_b", [P, CH, P], bf16)

        listing = early.enter_context(ExitStack())

        def sb(name, shape, dt=f32):
            return listing.enter_context(nc.sbuf_tensor(name, shape, dt))

        src_r = sb("src_r", [P, CH, P], i32)
        dst_r = sb("dst_r", [P, CH, P], i32)
        nxt_r = sb("nxt_r", [P, CH, P], i32)
        prv_r = sb("prv_r", [P, CH, P], i32)
        hi_r = sb("hi_r", [P, CH, P], i32)
        lo_r = sb("lo_r", [P, CH, P], i32)
        src_hi_r = sb("src_hi_r", [P, CH, P], i32)
        src_lo_r = sb("src_lo_r", [P, CH, P], i32)
        rows = [sb(f"rows{k}", [P, CH, P]) for k in range(COLS)]
        dst_f = sb("dst_f", [P, CH, P])
        nxt_f = sb("nxt_f", [P, CH, P])
        prv_f = sb("prv_f", [P, CH, P])
        new_f = sb("new_f", [P, CH, P])
        fst_f = sb("fst_f", [P, CH, P])
        open_row = sb("open_row", [1, CH * P + 1])
        open_in = sb("open_in", [1, CH * P])
        open_col = sb("open_col", [P, CH])
        listing.close()

        def sb(name, shape, dt=f32):
            return early.enter_context(nc.sbuf_tensor(name, shape, dt))

        xs = sb("xs", [P, XS, TB, D])

        digits = sb("digits", [P, 2, HCH * P], f16)
        gat_i = sb("gat_i", [P, XS, TB], i32)
        sca_i = sb("sca_i", [P, SC, TB], i32)
        ea = sb("ea", [P, 2, TB, ED])
        segq = sb("segq", [P, 2, W], bf16)
        highq = sb("highq", [P, HQ, W], f16)
        picks = sb("picks", [P, 2, HCH, W], f16)
        deg = sb("deg", [P, 2, 2 * TB])
        ds = sb("ds", [P, 2, 2 * TB])

        counting = early.enter_context(ExitStack())

        def sb(name, shape, dt=f32):
            return counting.enter_context(nc.sbuf_tensor(name, shape, dt))

        oh_hi = sb("oh_hi", [P, 2, TB, HIGH], f16)
        steps = sb("steps", [P, 2, TB, P], f16)
        cnt = sb("cnt", [P, HCH * P])
        sums_t = sb("sums_t", [P, HCH, P])
        cnt2 = sb("cnt2", [P, HCH, P])
        cnt_i = sb("cnt_i", [P, HCH * P], i32)
        digit_i = sb("digit_i", [P, 2, HCH * P], i32)
        counting.close()

        def sb(name, shape, dt=f32):
            return early.enter_context(nc.sbuf_tensor(name, shape, dt))

        picked = sb("picked", [P, 2, TB, P])
        eaT = sb("eaT", [ED, 2, W])
        he = sb("he", [P, 2, W])
        msg = sb("msg", [P, 2, TB, D])
        same = sb("same", [P, 2, TB, P])
        carry = sb("carry", [P, 2, TB, P])
        sums = sb("sums", [P, 2, D])
        scaled = sb("scaled", [P, 2, TB, D])

        early.close()

        def sb(name, shape, dt=f32):
            return persistent.enter_context(nc.sbuf_tensor(name, shape, dt))

        ag = sb("ag", [P, AR, BN, D])
        comb = sb("comb", [P, 2, TB, D])
        cT = sb("cT", [P, 2, W])
        hn = sb("hn", [P, 2, W])
        res = sb("res", [P, 2, TB, D])
        rw = sb("rw", [P, 4, TB, D])
        yn = sb("yn", [P, 2, TB, D])
        squares = sb("squares", [P, 4, TB - 1, D])
        last_squares = sb("last_squares", [P, 4, D])
        sq_sums = sb("sq_sums", [P, 2, 2 * TB])
        inverse = sb("inverse", [P, 2, 2 * TB])
        root = sb("root", [P, 2, 2 * TB])
        ysum = sb("ysum", [P, 2, TB])
        neg_mean = sb("neg_mean", [P, 2, TB])
        dev = sb("dev", [P, 4, TB, D])

        ps = [ctx.enter_context(nc.psum_tensor(f"bank{i}", [P, 512], f32)) for i in range(8)]

        zero_set = sem("zero_set")
        consts = sem("consts")
        ident_s = sem("ident_s")
        pads_set = sem("pads_set")
        rows_in = sem("rows_in")
        wts_in = sem("wts_in")
        bias_in = sem("bias_in")
        bias_ready = sem("bias_ready")
        agg_zeroed = sem("agg_zeroed")
        dchain = sem("dchain")
        pchain = sem("pchain")
        lasts_ready = sem("lasts_ready")
        lasts_turned = sem("lasts_turned")
        open_scanned = sem("open_scanned")
        open_turned = sem("open_turned")
        lists_ready = sem("lists_ready")
        dst_parts_ready = sem("dst_parts_ready")
        src_parts_ready = sem("src_parts_ready")
        src_ready = sem("src_ready")
        high_ready = sem("high_ready")
        seg_ready = sem("seg_ready")
        rows_ready = sem("rows_ready")
        cols_turned = sem("cols_turned")
        cols_ready = sem("cols_ready")
        seg_out = sem("seg_out")
        iota_set = sem("iota_set")
        eps_ready = sem("eps_ready")
        gidx_set = sem("gidx_set")
        high_hot = sem("high_hot")
        steps_ready = sem("steps_ready")
        counted = sem("counted")
        cnt_ready = sem("cnt_ready")
        cnt_turned = sem("cnt_turned")
        digits_ready = sem("digits_ready")
        high_out = sem("high_out")

        ea_in = sems("ea_in", 2)
        segq_in = sems("segq_in", 2)
        xs_in = sems("xs_in", XS)
        highq_in = sems("highq_in", HQ)
        picks_ready = sem("picks_ready")
        counts_picked = sem("counts_picked")
        deg_picked = sem("deg_picked")
        deg_floored = sem("deg_floored")
        deg_ready = sem("deg_ready")
        ds_ready = sem("ds_ready")
        scattered = sems("scattered", 2)
        gidx_ready = sem("gidx_ready")
        sidx_ready = sem("sidx_ready")
        eaT_done = sem("eaT_done")
        eaT_ready = sem("eaT_ready")
        h_done = sem("h_done")
        h_ready = sem("h_ready")
        m_done = sem("m_done")
        msg_ready = sem("msg_ready")
        masks_ready = sem("masks_ready")
        tile_summed = sem("tile_summed")
        sums_ready = sem("sums_ready")
        scaled_ready = sem("scaled_ready")

        xn_in = sems("xn_in", XR)
        ag_in = sems("ag_in", AR)
        out_sent = sems("out_sent", 2)
        comb_ready = sem("comb_ready")
        cT_done = sem("cT_done")
        cT_ready = sem("cT_ready")
        hn_done = sem("hn_done")
        hn_ready = sem("hn_ready")
        o_done = sem("o_done")
        res_ready = sem("res_ready")
        rw_ready = sem("rw_ready")
        ssq_ready = sem("ssq_ready")
        ssq_last = sem("ssq_last")
        var_last = sem("var_last")
        y_ready = sem("y_ready")
        mean_ready = sem("mean_ready")
        dev_ready = sem("dev_ready")
        var_ready = sem("var_ready")
        fin_ready = sem("fin_ready")
        fin_last = sem("fin_last")
        sp_passed = sem("sp_passed")
        pool_passed = sem("pool_passed")
        pe_passed = sem("pe_passed")
        sums_cleared = sem("sums_cleared")
        sums_scaled = sem("sums_scaled")
        inverse_ready = sem("inverse_ready")
        root_ready = sem("root_ready")

        block = ctx.enter_context(nc.Block())

        def at(n):
            return n.value() if isinstance(n, Count) else n

        def need(eng, s, value):
            if isinstance(value, Count):
                assert value.per * value.first + value.base > 0
            if not (isinstance(value, int) and value <= 0):
                eng.wait_ge(s, at(value))

        def apart(eng, passed):
            eng.sem_inc(passed, 1)

        def run(eng, total, unroll, step, tail=0, head=1, peel=0, begin=0):
            rounds = total // unroll - peel
            for n in range(begin, head * unroll):
                step(n, n % unroll)
            with eng.Fori(head, rounds) as i:
                for u in range(unroll):
                    step(Count(i, unroll, u, head), u)
            for n in range(rounds * unroll, total + tail):
                step(n, n % unroll)

        def live(n, total):
            return not isinstance(n, int) or 0 <= n < total

        def block_loads(B, ring):
            return (B // ring + 1 + (isinstance(B, int) and B == BLOCKS - 1)) * 16

        def place(n, u):
            return n // SPB, (u // SPB) % XR, (u // SPB) % AR, (u % SPB) * TB

        ZERO_COLS = 2 * BN
        ZERO_FIRST = 8
        ZERO_DMAS = -(-NPP // ZERO_COLS) + 1

        ROW_DMAS = 14
        WEIGHTS = 8

        def index_rows(eng, tile, a, off):
            lo = 1 if off < 0 else 0
            if off < 0:
                eng.dma_start(tile[0:1, 0, 1:P], a[0:P - 1].rearrange("(o c) -> o c", o=1)).then_inc(rows_in, 16)
                eng.dma_start(tile[1:P, 0, :], a[P + off:P * P + off].rearrange("(p c) -> p c", c=P)).then_inc(rows_in, 16)
            span = P * P * (CH - 1)
            eng.dma_start(tile[:, lo:CH - 1, :],
                          a[lo * P * P + off:span + off].rearrange("(k p c) -> p k c", p=P, c=P)).then_inc(rows_in, 16)
            more = FULL - P * (CH - 1)
            eng.dma_start(tile[0:more, CH - 1, :],
                          a[span + off:FULL * P + off].rearrange("(p c) -> p c", c=P)).then_inc(rows_in, 16)
            eng.dma_start(tile[more:more + 1, CH - 1, 0:REST - off],
                          a[FULL * P + off:E].rearrange("(o c) -> o c", o=1)).then_inc(rows_in, 16)

        x_main = x[0:NPP * P, :].rearrange("(p i) d -> p i d", p=P)
        ag_main = agg_d[0:NPP * P, :].rearrange("(p i) d -> p i d", p=P)
        out_main = out[0:NPP * P, :].rearrange("(p i) d -> p i d", p=P)

        @block.sync
        def _(sp):
            sp.wait_ge(pads_set, 4)
            for tile, a, off in ((dst_r, dst, 0), (nxt_r, dst, 1)):
                index_rows(sp, tile, a, off)
            for o, i in ((w1e[:, :], W1e), (w2e[:, :], W2e), (w1n[:, :], W1n), (w2n[:, :], W2n),
                         (b1e_c[:, :], b1e.rearrange("(p o) -> p o", o=1)),
                         (b1n_c[:, :], b1n.rearrange("(p o) -> p o", o=1)),
                         (rms_b[:, :], rms_w.rearrange("(o d) -> o d", o=1).partition_broadcast(P)),
                         (eps1[:, :], gin_eps.rearrange("(o d) -> o d", o=1).partition_broadcast(P))):
                sp.dma_start(o, i).then_inc(wts_in, 16)
            sp.wait_ge(rows_in, 16 * ROW_DMAS)
            sp.wait_ge(wts_in, 16 * WEIGHTS)
            sp.wait_ge(zero_set, 1)

            def zero(first, last):
                for c in range(first * ZERO_COLS, min(last * ZERO_COLS, NPP), ZERO_COLS):
                    w = min(ZERO_COLS, NPP - c)
                    sp.dma_start(ag_main[:, c:c + w, :],
                                 on.rearrange("p o i d -> p (o i) d")[:, 0:w, :]).then_inc(agg_zeroed, 16)

            zero(0, ZERO_FIRST)
            sp.dma_start(agg_d[NPP * P:N, :], on[0:NREM, 0, 0, :]).then_inc(agg_zeroed, 16)

            sp.wait_ge(seg_ready, 1)
            sp.dma_start(seg_d[:].rearrange("(k p c) -> p k c", p=P, c=P), seg_b[:, :, :]).then_inc(seg_out, 16)
            sp.wait_ge(high_ready, 1)
            sp.dma_start(high_d[:].rearrange("(k p c) -> p k c", p=P, c=P), high_b[:, :, :]).then_inc(high_out, 16)
            sp.wait_ge(seg_out, 16)
            sp.wait_ge(high_out, 16)

            def high_load(b, s):
                need(sp, picks_ready, b - HQ + 1)
                apart(sp, sp_passed)
                sp.dma_start(highq[:, s, :],
                             high_d[bass.ds(at(b * W), W)].rearrange("(o c) -> o c", o=1).partition_broadcast(P)
                             ).then_inc(highq_in[s], 16)

            def edge_loads(b, u):
                s = u % 2
                need(sp, eaT_done, b - 1)
                apart(sp, sp_passed)
                if isinstance(b, int) and b * W + W > E:
                    whole = FULL - b * TB
                    sp.dma_start(ea[:, s, 0:whole, :],
                                 edge_attr[b * W:FULL * P, :].rearrange("(j p) d -> p j d", p=P)).then_inc(ea_in[s], 16)
                    sp.dma_start(ea[0:REST, s, whole, :], edge_attr[FULL * P:E, :]).then_inc(ea_in[s], 16)
                else:
                    sp.dma_start(ea[:, s, :, :],
                                 edge_attr[bass.ds(at(b * W), W), :].rearrange("(j p) d -> p j d", p=P)).then_inc(ea_in[s], 16)
                need(sp, masks_ready, b - 1)
                apart(sp, sp_passed)
                sp.dma_start(segq[:, s, :],
                             seg_d[bass.ds(at(b * W), W)].rearrange("(o c) -> o c", o=1).partition_broadcast(P)
                             ).then_inc(segq_in[s], 16)

            def edge_and_high_loads(b, u):
                edge_loads(b, u)
                if live(b + HQ, BATCHES):
                    high_load(b + HQ, u % HQ)

            for b in range(HQ):
                high_load(b, b)
            for b in range(2):
                edge_loads(b, b)
            zero(ZERO_FIRST, NPP)
            for b in range(2):
                high_load(b + HQ, b)
            run(sp, BATCHES, HQ, edge_and_high_loads, peel=1, begin=2)

            def load_block(tile, slot, whole, view, B, landed):
                if isinstance(B, int) and B == BLOCKS - 1:
                    sp.dma_start(tile[:, slot, 0:LASTC, :], view[:, B * BN:NPP, :]).then_inc(landed, 16)
                    sp.dma_start(tile[0:NREM, slot, LASTC, :], whole[NPP * P:N, :]).then_inc(landed, 16)
                else:
                    sp.dma_start(tile[:, slot, :, :], view[:, bass.ds(at(B * BN), BN), :]).then_inc(landed, 16)

            for B in range(XR):
                load_block(xn, B, x, x_main, B, xn_in[B])
            for s in range(2):
                sp.wait_ge(scattered[s], 16 * TB * (BATCHES // 2))

            def node_block(B, u):
                if live(B, BLOCKS):
                    need(sp, comb_ready, (B - AR + 1) * SPB)
                    load_block(ag, u % AR, agg_d, ag_main, B, ag_in[u % AR])
                    if not isinstance(B, int) or B >= XR:
                        sp.wait_ge(y_ready, at((B - XR + 1) * SPB))
                        load_block(xn, u % XR, x, x_main, B, xn_in[u % XR])
                C, o = B - XR, (u - XR) % 2
                if live(C, BLOCKS):
                    need(sp, fin_ready, (C + 1) * SPB)
                    need(sp, fin_last, (C + 1) * SPB)
                    if isinstance(C, int) and C == BLOCKS - 1:
                        sp.dma_start(out_main[:, C * BN:NPP, :], on[:, o, 0:LASTC, :]).then_inc(out_sent[o], 16)
                        sp.dma_start(out[NPP * P:N, :], on[0:NREM, o, LASTC, :]).then_inc(out_sent[o], 16)
                    else:
                        sp.dma_start(out_main[:, bass.ds(at(C * BN), BN), :], on[:, o, :, :]).then_inc(out_sent[o], 16)

            run(sp, BLOCKS, XR, node_block, tail=XR)
            for o in range(2):
                blocks = len(range(o, BLOCKS, 2))
                sp.wait_ge(out_sent[o], 16 * (blocks + int((BLOCKS - 1) % 2 == o)))

        @block.gpsimd
        def _(pool):
            for t, v in ((dst_r, NO_NODE), (nxt_r, NO_NODE), (prv_r, NO_NODE), (src_r, 0)):
                pool.memset(t[:, :, :], v).then_inc(pads_set, 1)
            pool.memset(ident[:, :], 0.0).then_inc(pchain, 1)
            pool.wait_ge(pchain, 1)
            pool.affine_select(out=ident[:, :], in_=ident[:, :], compare_op=ALU.not_equal, fill=1.0, base=0,
                               pattern=[[-1, P]], channel_multiplier=1).then_inc(ident_s, 1)
            pool.iota(iota_i[:, :], pattern=[[1, HIGH]], base=0, channel_multiplier=0).then_inc(consts, 1)
            pool.iota(gidx_i[:, :, :], pattern=[[P * P, CH], [1, P]], base=0, channel_multiplier=P).then_inc(consts, 1)
            pool.iota(high_i[:, :], pattern=[[P, HCH]], base=0, channel_multiplier=1).then_inc(consts, 1)
            pool.memset(ones[:, :], 1.0).then_inc(consts, 1)
            pool.memset(ones_b[:, :], 1.0).then_inc(consts, 1)
            pool.memset(cnt[:, :], 0.0).then_inc(consts, 1)
            pool.memset(ea[:, :, :, :], 0.0).then_inc(consts, 1)
            pool.memset(on[:, :, :, :], 0.0).then_inc(zero_set, 1)

            links = [1]

            def link(ins):
                links[0] += 1
                ins.then_inc(pchain, 1)
                pool.wait_ge(pchain, links[0])

            pool.wait_ge(bias_in, 32)
            pool.wait_ge(ident_s, 1)
            link(pool.memset(bias_s[:, :, :], 0.0))
            for k in range(3):
                link(pool.tensor_copy(bias_p[:, :, :], bias_f[:, :, :]))
                link(pool.tensor_copy(bias_r[:, :, :], bias_p[:, :, :]))
                pool.tensor_tensor(bias_f[:, :, :], bias_f[:, :, :], bias_r[:, :, :], ALU.subtract)
                link(pool.tensor_tensor(bias_m[:, :, :], bias_r[:, :, :],
                                        ident[:, k:k + 1].unsqueeze(1).to_broadcast([P, 2, D]), ALU.mult))
                link(pool.tensor_tensor(bias_s[:, :, :], bias_s[:, :, :], bias_m[:, :, :], ALU.add))
            for j in range(TB):
                last = pool.tensor_copy(bias[:, :, j, :], bias_s[:, :, :])
            last.then_inc(bias_ready, 1)

            def gather(b, u):
                pool.wait_ge(gidx_ready, at(b + 1))
                need(pool, msg_ready, b - XS + 1)
                apart(pool, pool_passed)
                for j in range(TB):
                    pool.indirect_dma_start(out=xs[:, u, j, :], out_offset=None, in_=x,
                                            in_offset=bass.IndirectOffsetOnAxis(ap=gat_i[:, u, j:j + 1], axis=0)
                                            ).then_inc(xs_in[u], 16)

            def scatter(b, u):
                s = u % 2
                if isinstance(b, int) and b == 0:
                    pool.wait_ge(agg_zeroed, ZERO_DMAS * 16)
                pool.wait_ge(sidx_ready, at(b + 1))
                for j in range(TB):
                    pool.wait_ge(scaled_ready, at(b * TB + j + 1))
                    apart(pool, pool_passed)
                    pool.indirect_dma_start(out=agg_rows,
                                            out_offset=bass.IndirectOffsetOnAxis(ap=sca_i[:, u % SC, j:j + 1], axis=0),
                                            in_=scaled[:, s, j, :], in_offset=None,
                                            bounds_check=N - 1, oob_is_err=False).then_inc(scattered[s], 16)

            def round_trip(r, gathers, shift):
                for k in range(ROUND):
                    scatter(r * ROUND + k, k)
                    for g in range(min(k * gathers // SPREAD, gathers), min((k + 1) * gathers // SPREAD, gathers)):
                        gather(r * ROUND_IN + XS + shift + g, (shift + g) % XS)

            pool.wait_ge(cols_turned, COLS)
            for b in range(XS):
                gather(b, b)
            round_trip(0, FIRST_IN, 0)
            with pool.Fori(1, ROUNDS) as i:
                round_trip(Count(i, 1, 0), ROUND_IN, FIRST_IN - ROUND_IN)
            for b in range(ROUNDS * ROUND, BATCHES):
                scatter(b, b % ROUND)

            def node_step(n, u):
                m, s = n - 5, (u - 5) % 4
                if live(m, STEPS):
                    pool.wait_ge(res_ready, at(m + 1))
                    need(pool, y_ready, m - 3)
                    pool.tensor_tensor(rw[:, s, :, :], res[:, s % 2, :, :],
                                       rms_b[:, :].unsqueeze(1).to_broadcast([P, TB, D]), ALU.mult).then_inc(rw_ready, 1)
                m, s = n - 8, (u - 8) % 4
                if live(m, STEPS):
                    pool.wait_ge(mean_ready, at(m + 1))
                    need(pool, fin_ready, m - 3)
                    need(pool, fin_last, m - 3)
                    pool.tensor_tensor(dev[:, s, :, :], yn[:, s % 2, :, :],
                                       neg_mean[:, s % 2, :].unsqueeze(2).to_broadcast([P, TB, D]),
                                       ALU.add).then_inc(dev_ready, 1)
                m, s = n - 11, (u - 11) % 4
                if live(m, STEPS):
                    B, o, h = m // SPB, ((u - 11) // SPB) % 2, ((u - 11) % SPB) * TB
                    pool.wait_ge(root_ready, at(m + VAR_LAG + 1))
                    pool.wait_ge(dev_ready, at(m + 1))
                    if (u - 11) % SPB == 0:
                        need(pool, out_sent[o], B // 2 * 16)
                    tiles = TB - s % 2
                    pool.tensor_tensor(on[:, o, h:h + tiles, :], dev[:, s, 0:tiles, :],
                                       root[:, s % 2, TB:TB + tiles].unsqueeze(2).to_broadcast([P, tiles, D]),
                                       ALU.mult).then_inc(fin_ready, 1)

            run(pool, STEPS, SPB * XR, node_step, tail=11)

        @block.scalar
        def _(act):
            for k, b2 in ((0, b2e), (1, b2n)):
                act.dma_start(bias_f[:, k, :], b2.rearrange("(o d) -> o d", o=1).partition_broadcast(P)
                              ).then_inc(bias_in, 16)
            act.wait_ge(pads_set, 4)
            for tile, a, off in ((prv_r, dst, -1), (src_r, src, 0)):
                index_rows(act, tile, a, off)

            act.wait_ge(rows_in, 16 * ROW_DMAS)
            for f, r in ((dst_f, dst_r), (prv_f, prv_r), (nxt_f, nxt_r)):
                act.activation(f[:, :, :], r[:, :, :], ACT.Copy).then_inc(lists_ready, 1)
            act.activation(rows[SRC][:, :, :], src_r[:, :, :], ACT.Copy).then_inc(src_ready, 1)

            def column(k):
                act.wait_ge(cols_turned, k + 1)
                act.activation(cols[k][:, :], ps[4 + k % 2][:, :], ACT.Copy).then_inc(cols_ready, 1)

            column(HI)
            column(STEP)
            act.wait_ge(src_parts_ready, 1)
            act.activation(rows[SRC_LO][:, :, :], src_lo_r[:, :, :], ACT.Copy).then_inc(src_ready, 1)
            act.activation(high_b[:, :, :], src_hi_r[:, :, :], ACT.Copy).then_inc(high_ready, 1)
            for k in range(SRC, COLS):
                column(k)

            act.wait_ge(cols_ready, COLS)
            act.wait_ge(iota_set, 1)

            def count_step(b, u):
                s = u % 2
                need(act, counted, b - 1)
                for j in range(TB):
                    act.activation(steps[:, s, j, :], iota_h[:, 0:P], ACT.Sign,
                                   bias=cols[STEP][:, bass.ds(at(b * TB + j), 1)]).then_inc(steps_ready, 1)

            run(act, BATCHES, 2, count_step)
            def tile_out(b, u, j):
                s = u % 2
                t = b * TB + j
                act.wait_ge(tile_summed, at(t + 1))
                act.activation(sums[:, j % 2, :], ps[6 + j % 2][:, 0:D], ACT.Copy).then_inc(sums_ready, 1)
                if j == 0:
                    act.wait_ge(ds_ready, at(b + 1))
                    need(act, scattered[s], b // 2 * 16 * TB)
                act.activation(scaled[:, s, j, :], ps[6 + j % 2][:, 0:D], ACT.Copy,
                               scale=ds[:, s, TB + j:TB + j + 1]).then_inc(scaled_ready, 1)

            def edge_step(b, u):
                s = u % 2
                if live(b, BATCHES):
                    act.wait_ge(eaT_done, at(b + 1))
                    need(act, h_done, b - 1)
                    act.activation(eaT[:, s, :], ps[2][0:ED, :], ACT.Copy).then_inc(eaT_ready, 1)
                if live(b - 1, BATCHES):
                    tile_out(b - 1, u - 1, 0)
                if live(b, BATCHES):
                    act.wait_ge(deg_ready, at(b + 1))
                    need(act, masks_ready, b - 1)
                    need(act, scaled_ready, (b - 1) * TB)
                    act.activation(ds[:, s, :], deg[:, s, :], ACT.Sqrt).then_inc(ds_ready, 1)
                    act.wait_ge(h_done, at(b + 1))
                    need(act, m_done, b - 1)
                    act.activation(he[:, s, :], ps[3][:, :], ACT.Relu, bias=b1e_c[:, 0:1]).then_inc(h_ready, 1)
                if live(b - 1, BATCHES):
                    for j in range(1, TB):
                        tile_out(b - 1, u - 1, j)
            run(act, BATCHES, 2, edge_step, tail=1, head=2, peel=1)

            def node_step(n, u):
                m, s = n - 7, (u - 7) % 2
                if live(m, STEPS + VAR_LAG):
                    act.wait_ge(inverse_ready, at(m + 1))
                    need(act, y_ready, min(m - 1, STEPS) if isinstance(m, int) else m - 1)
                    need(act, fin_ready, m - 1 - VAR_LAG)
                    need(act, fin_last, m - 1 - VAR_LAG)
                    act.activation(root[:, s, :], inverse[:, s, :], ACT.Sqrt).then_inc(root_ready, 1)
                m, s = n - 2, (u - 2) % 2
                if live(m, STEPS):
                    act.wait_ge(cT_done, at(m + 1))
                    need(act, hn_done, m - 1)
                    act.activation(cT[:, s, :], ps[s][:, :], ACT.Copy).then_inc(cT_ready, 1)
                m, s = n - 3, (u - 3) % 2
                if live(m, STEPS):
                    act.wait_ge(hn_done, at(m + 1))
                    need(act, o_done, m - 1)
                    act.activation(hn[:, s, :], ps[2 + s][:, :], ACT.Relu, bias=b1n_c[:, 0:1]).then_inc(hn_ready, 1)
                m, s = n - 5, (u - 5) % 2
                if live(m, STEPS):
                    act.wait_ge(res_ready, at(m + 1))
                    need(act, sums_scaled, m - 1)
                    for j in range(TB - 1):
                        last = act.activation(squares[:, s, j, :], res[:, s, j, :], ACT.Square,
                                              accum_out=sq_sums[:, s, j:j + 1])
                    last.then_inc(ssq_ready, 1)
                m, s = n - 9, (u - 9) % 4
                if live(m, STEPS):
                    act.wait_ge(dev_ready, at(m + 1))
                    act.wait_ge(sums_scaled, at(m + VAR_LAG - 1))
                    for j in range(TB - 1):
                        last = act.activation(squares[:, 2 + s % 2, j, :], dev[:, s, j, :], ACT.Square,
                                              accum_out=sq_sums[:, s % 2, TB + j:TB + j + 1])
                    last.then_inc(var_ready, 1)
                m, s = n - 11, (u - 11) % 4
                if live(m, STEPS):
                    B, o, h = m // SPB, ((u - 11) // SPB) % 2, ((u - 11) % SPB) * TB
                    act.wait_ge(root_ready, at(m + VAR_LAG + 1))
                    if s == 0:
                        need(act, out_sent[o], B // 2 * 16)
                    if s % 2:
                        act.wait_ge(dev_ready, at(m + 1))
                        act.activation(on[:, o, h + TB - 1, :], dev[:, s, TB - 1, :], ACT.Copy,
                                       scale=root[:, s % 2, 2 * TB - 1:2 * TB]).then_inc(fin_last, 1)
                    else:
                        act.sem_inc(fin_last, 1)

            run(act, STEPS, SPB * XR, node_step, tail=11)

        @block.vector
        def _(dve):
            done = [0]

            def link(ins):
                done[0] += 1
                ins.then_inc(dchain, 1)
                dve.wait_ge(dchain, done[0])

            dve.wait_ge(consts, 7)
            dve.tensor_copy(iota_h[:, :], iota_i[:, :]).then_inc(iota_set, 1)
            dve.tensor_copy(high_no[:, :], high_i[:, :])
            dve.tensor_copy(gidx[:, :, :], gidx_i[:, :, :]).then_inc(gidx_set, 1)
            dve.wait_ge(gidx_set, 1)
            dve.wait_ge(rows_in, 16 * ROW_DMAS)
            dve.tensor_scalar(hi_r[:, :, :], dst_r[:, :, :], 7, None, ALU.arith_shift_right)
            link(dve.tensor_scalar(lo_r[:, :, :], dst_r[:, :, :], P - 1, None, ALU.bitwise_and))
            dve.tensor_copy(rows[HI][:, :, :], hi_r[:, :, :])
            dve.tensor_scalar(rows[STEP][:, :, :], lo_r[:, :, :], -1.0, 0.5, ALU.mult, ALU.add).then_inc(dst_parts_ready, 1)
            dve.tensor_scalar(src_hi_r[:, :, :], src_r[:, :, :], 7, None, ALU.arith_shift_right)
            dve.tensor_scalar(src_lo_r[:, :, :], src_r[:, :, :], P - 1, None, ALU.bitwise_and).then_inc(src_parts_ready, 1)
            dve.wait_ge(lists_ready, 3)
            dve.tensor_tensor(nxt_f[:, :, :], dst_f[:, :, :], nxt_f[:, :, :], ALU.is_equal)
            link(dve.tensor_tensor(new_f[:, :, :], dst_f[:, :, :], prv_f[:, :, :], ALU.not_equal))
            dve.scalar_tensor_tensor(rows[SCAT][:, :, :], nxt_f[:, :, :], SKIP, dst_f[:, :, :], ALU.mult, ALU.add)
            link(dve.scalar_tensor_tensor(fst_f[:, :, :], gidx[:, :, :], 1.0, new_f[:, :, :], ALU.add, ALU.mult))
            for k in range(CH):
                dve.tensor_tensor_scan(rows[SEG][:, k, :], ones[:, :], new_f[:, k, :], 0.0, ALU.mult, ALU.add)
                last = dve.tensor_tensor_scan(prv_f[:, k, :], ones[:, :], fst_f[:, k, :], 0.0, ALU.mult, ALU.max)
            link(last)
            dve.tensor_copy(seg_b[:, :, :], rows[SEG][:, :, :]).then_inc(seg_ready, 1)
            dve.tensor_copy(open_col[:, :], prv_f[:, :, P - 1]).then_inc(lasts_ready, 1)
            dve.memset(open_row[:, 0:1], 0.0)
            dve.wait_ge(lasts_turned, 1)
            link(dve.tensor_copy(open_in[:, :], ps[6][0:1, :]))
            link(dve.tensor_tensor_scan(open_row[:, 1:CH * P + 1], open_in[:, :], open_in[:, :], 0.0,
                                        ALU.max, ALU.max))
            dve.sem_inc(open_scanned, 1)
            dve.wait_ge(open_turned, 1)
            link(dve.tensor_copy(open_col[:, :], ps[7][:, 0:CH]))
            for k in range(CH):
                last = dve.tensor_scalar(fst_f[:, k, :], prv_f[:, k, :], open_col[:, k:k + 1], None, ALU.max)
            link(last)
            link(dve.scalar_tensor_tensor(new_f[:, :, :], fst_f[:, :, :], -1.0, gidx[:, :, :], ALU.mult, ALU.add))
            dve.tensor_scalar(rows[LEN][:, :, :], new_f[:, :, :], 2.0, None, ALU.add).then_inc(rows_ready, 1)

            dve.wait_ge(wts_in, 16 * WEIGHTS)
            dve.tensor_scalar(eps1[:, :], eps1[:, :], 1.0, None, ALU.add).then_inc(eps_ready, 1)
            dve.wait_ge(cols_ready, SRC + 1)
            dve.tensor_copy(gat_i[:, :, :].rearrange("p b j -> p (b j)"), cols[SRC][:, 0:XS * TB]
                            ).then_inc(gidx_ready, XS)

            def count_step(b, u):
                s = u % 2
                need(dve, counted, b - 1)
                for j in range(TB):
                    dve.tensor_scalar(oh_hi[:, s, j, :], iota_h[:, :], cols[HI][:, bass.ds(at(b * TB + j), 1)], None,
                                      ALU.is_equal).then_inc(high_hot, 1)

            run(dve, BATCHES, 2, count_step)
            dve.wait_ge(counted, BATCHES)
            dve.tensor_copy(cnt[:, 0:512], ps[0][:, :])
            dve.tensor_copy(cnt[:, 512:HIGH], ps[1][:, 0:HIGH - 512]).then_inc(cnt_ready, 1)

            def pick_columns(b, u):
                s, q = u % 2, u % HQ
                dve.wait_ge(highq_in[q], at((b // HQ + 1) * 16))
                need(dve, counts_picked, b - 1)
                for c in range(HCH):
                    last = dve.tensor_scalar(picks[:, s, c, :], highq[:, q, :], high_no[:, c:c + 1], None, ALU.is_equal)
                last.then_inc(picks_ready, 1)

            pick_columns(0, 0)
            dve.wait_ge(cnt_turned, 1)
            sums_flat = sums_t[:, :, :].rearrange("p c l -> p (c l)")
            dve.tensor_copy(sums_flat[:, 0:512], ps[4][:, :])
            link(dve.tensor_copy(sums_flat[:, 512:HCH * P], ps[5][:, 0:HCH * P - 512]))
            dve.tensor_tensor(cnt2[:, :, 0], sums_t[:, :, 0], sums_t[:, :, P - 1], ALU.add)
            link(dve.tensor_tensor(cnt2[:, :, 1:P], sums_t[:, :, 1:P], sums_t[:, :, 0:P - 1], ALU.subtract))
            link(dve.tensor_scalar(cnt_i[:, :], cnt2[:, :, :].rearrange("p c l -> p (c l)"), 0.5, None, ALU.mult))
            dve.tensor_scalar(digit_i[:, 0, :], cnt_i[:, :], DIGIT - 1, None, ALU.bitwise_and)
            link(dve.tensor_scalar(digit_i[:, 1, :], cnt_i[:, :], 65536 - DIGIT, None, ALU.bitwise_and))
            dve.tensor_copy(digits[:, :, :], digit_i[:, :, :]).then_inc(digits_ready, 1)
            pick_columns(1, 1)

            def degrees(b, s):
                dve.wait_ge(counts_picked, at(b + 1))
                need(dve, ds_ready, b - 1)
                dve.tensor_copy(deg[:, s, TB:2 * TB], cols[LEN][:, bass.ds(at(b * TB), TB)])
                for j in range(TB):
                    last = dve.scalar_tensor_tensor(picked[:, s, j, :], iota_h[:, 0:P],
                                                    cols[SRC_LO][:, bass.ds(at(b * TB + j), 1)],
                                                    ps[s][:, j * P:(j + 1) * P], ALU.is_equal, ALU.mult,
                                                    accum_out=deg[:, s, j:j + 1])
                last.then_inc(deg_picked, 1)
                dve.wait_ge(deg_picked, at(b + 1))
                dve.tensor_scalar(deg[:, s, :], deg[:, s, :], 1.0, None, ALU.max).then_inc(deg_floored, 1)
                dve.wait_ge(deg_floored, at(b + 1))
                dve.reciprocal(deg[:, s, :], deg[:, s, :]).then_inc(deg_ready, 1)

            def edge_step(b, u):
                s = u % 2
                need(dve, scattered[s], (b // 2 - SC // 2 + 1) * 16 * TB)
                dve.tensor_copy(sca_i[:, u % SC, :], cols[SCAT][:, bass.ds(at(b * TB), TB)]).then_inc(sidx_ready, 1)
                dve.wait_ge(segq_in[s], at((b // 2 + 1) * 16))
                need(dve, tile_summed, (b - 1) * TB)
                dve.tensor_scalar(carry[:, s, :, :].rearrange("p j c -> p (j c)"), segq[:, s, :], 0.0,
                                  ident[:, P - 1:P], ALU.is_equal, ALU.mult)
                dve.wait_ge(ds_ready, at(b + 1))
                for j in range(TB):
                    last = dve.tensor_scalar(same[:, s, j, :], segq[:, s, j * P:(j + 1) * P],
                                             cols[SEG][:, bass.ds(at(b * TB + j), 1)], ds[:, s, j:j + 1],
                                             ALU.is_equal, ALU.mult)
                last.then_inc(masks_ready, 1)
                if live(b + 2, BATCHES):
                    pick_columns(b + 2, u + 2)
                dve.wait_ge(xs_in[u], at((b // XS + 1) * 16 * TB))
                dve.wait_ge(m_done, at(b + 1))
                dve.tensor_tensor(msg[:, s, :, :].rearrange("p j d -> p (j d)"), ps[4 + s][:, :],
                                  xs[:, u, :, :].rearrange("p j d -> p (j d)"), ALU.add).then_inc(msg_ready, 1)
                if live(b + XS, BATCHES):
                    dve.tensor_copy(gat_i[:, u, :], cols[SRC][:, bass.ds(at((b + XS) * TB), TB)]
                                    ).then_inc(gidx_ready, 1)
                if live(b + 1, BATCHES):
                    degrees(b + 1, 1 - s)

            dve.wait_ge(cols_ready, COLS)
            degrees(0, 0)
            run(dve, BATCHES, XS, edge_step, peel=1)

            dve.wait_ge(eps_ready, 1)
            dve.memset(epsilons[:, 0:TB], RMS_EPS)
            dve.memset(epsilons[:, TB:2 * TB], LN_EPS)
            dve.memset(sq_sums[:, :, :], 0.0).then_inc(sums_cleared, 1)
            dve.wait_ge(sums_cleared, 1)

            def node_step(n, u):
                m, s = n - 6, (u - 6) % 2
                if live(m, STEPS):
                    dve.wait_ge(res_ready, at(m + 1))
                    need(dve, sums_scaled, m - 1)
                    dve.scalar_tensor_tensor(last_squares[:, s, :], res[:, s, TB - 1, :], 1.0, res[:, s, TB - 1, :],
                                             ALU.mult, ALU.mult, accum_out=sq_sums[:, s, TB - 1:TB]).then_inc(ssq_last, 1)
                m, s, r = n - 10, (u - 10) % 2, (u - 10) % 4
                if live(m, STEPS):
                    dve.wait_ge(dev_ready, at(m + 1))
                    dve.wait_ge(sums_scaled, at(m + VAR_LAG - 1))
                    dve.scalar_tensor_tensor(last_squares[:, 2 + s, :], dev[:, r, TB - 1, :], 1.0, dev[:, r, TB - 1, :],
                                             ALU.mult, ALU.mult, accum_out=sq_sums[:, s, 2 * TB - 1:2 * TB]
                                             ).then_inc(var_last, 1)
                m, s = n - 7, (u - 7) % 4
                if live(m, STEPS):
                    _, xsl, _, h = place(m, u - 7)
                    dve.wait_ge(root_ready, at(m + 1))
                    dve.wait_ge(rw_ready, at(m + 1))
                    need(dve, dev_ready, m - 1)
                    for j in range(TB):
                        last = dve.scalar_tensor_tensor(yn[:, s % 2, j, :], rw[:, s, j, :], root[:, s % 2, j:j + 1],
                                                        xn[:, xsl, h + j, :], ALU.mult, ALU.add,
                                                        accum_out=ysum[:, s % 2, j:j + 1])
                    last.then_inc(y_ready, 1)
                m, s = n - 6, (u - 6) % 2
                if live(m, STEPS + VAR_LAG):
                    if live(m, STEPS):
                        dve.wait_ge(ssq_last, at(m + 1))
                        dve.wait_ge(ssq_ready, at(m + 1))
                    need(dve, var_last, m - VAR_LAG + 1)
                    need(dve, var_ready, m - VAR_LAG + 1)
                    need(dve, root_ready, m - 1)
                    dve.scalar_tensor_tensor(inverse[:, s, :], sq_sums[:, s, :], 1.0 / D, epsilons[:, :],
                                             ALU.mult, ALU.add).then_inc(sums_scaled, 1)
                s = u % 2
                if live(n, STEPS):
                    B, xsl, asl, h = place(n, u)
                    dve.wait_ge(xn_in[xsl], at(block_loads(B, XR)))
                    dve.wait_ge(ag_in[asl], at(block_loads(B, AR)))
                    need(dve, cT_done, n - 1)
                    dve.scalar_tensor_tensor(comb[:, s, :, :], xn[:, xsl, h:h + TB, :], eps1[:, 0:1],
                                             ag[:, asl, h:h + TB, :], ALU.mult, ALU.add).then_inc(comb_ready, 1)
                m, s = n - 6, (u - 6) % 2
                if live(m, STEPS + VAR_LAG):
                    dve.wait_ge(sums_scaled, at(m + 1))
                    dve.reciprocal(inverse[:, s, :], inverse[:, s, :]).then_inc(inverse_ready, 1)
                m, s = n - 7, (u - 7) % 2
                if live(m, STEPS):
                    dve.wait_ge(y_ready, at(m + 1))
                    need(dve, dev_ready, m - 1)
                    dve.tensor_scalar(neg_mean[:, s, :], ysum[:, s, :], -1.0 / D, None,
                                      ALU.mult).then_inc(mean_ready, 1)
                m, s = n - 4, (u - 4) % 2
                if live(m, STEPS):
                    _, xsl, _, h = place(m, u - 4)
                    dve.wait_ge(o_done, at(m + 1))
                    need(dve, ssq_ready, m - 1)
                    need(dve, ssq_last, m - 1)
                    need(dve, rw_ready, m - 1)
                    dve.tensor_tensor(res[:, s, :, :].rearrange("p j d -> p (j d)"), ps[4 + s][:, :],
                                      xn[:, xsl, h:h + TB, :].rearrange("p j d -> p (j d)"),
                                      ALU.add).then_inc(res_ready, 1)

            run(dve, STEPS, SPB * XR, node_step, tail=10)

        @block.tensor
        def _(pe):
            def turn(k):
                need(pe, cols_ready, k - 1)
                for c in range(CH):
                    last = pe.transpose(ps[4 + k % 2][:, c * P:(c + 1) * P], rows[k][:, c, :], ident[:, :])
                last.then_inc(cols_turned, 1)

            pe.wait_ge(ident_s, 1)
            pe.wait_ge(consts, 7)
            pe.wait_ge(dst_parts_ready, 1)
            turn(HI)
            turn(STEP)
            pe.wait_ge(lasts_ready, 1)
            for k in range(CH):
                last = pe.transpose(ps[6][0:1, k * P:(k + 1) * P], open_col[:, k:k + 1], ident[:, :])
            last.then_inc(lasts_turned, 1)
            pe.wait_ge(src_ready, 2)
            turn(SRC)
            turn(SRC_LO)
            pe.wait_ge(open_scanned, 1)
            for k in range(CH):
                last = pe.transpose(ps[7][:, k:k + 1], open_row[0:1, k * P:(k + 1) * P], ident[0:1, 0:1])
            last.then_inc(open_turned, 1)
            pe.wait_ge(rows_ready, 1)
            for k in range(SCAT, COLS):
                turn(k)

            def count_step(b, u):
                s = u % 2
                for j in range(TB):
                    pe.wait_ge(high_hot, at(b * TB + j + 1))
                    pe.wait_ge(steps_ready, at(b * TB + j + 1))
                    first = isinstance(b, int) and b == 0 and j == 0
                    end = isinstance(b, int) and b == BATCHES - 1 and j == TB - 1
                    pe.matmul(ps[0][:, :], steps[:, s, j, :], oh_hi[:, s, j, 0:512], start=first, stop=end)
                    last = pe.matmul(ps[1][:, 0:HIGH - 512], steps[:, s, j, :], oh_hi[:, s, j, 512:HIGH],
                                     start=first, stop=end)
                last.then_inc(counted, 1)

            run(pe, BATCHES, 2, count_step, peel=1)
            pe.wait_ge(cnt_ready, 1)
            pe.wait_ge(cols_ready, COLS)
            for c in range(HCH):
                last = pe.transpose(ps[4 + c // 4][:, (c % 4) * P:(c % 4 + 1) * P], cnt[:, c * P:(c + 1) * P],
                                    ident[:, :])
            last.then_inc(cnt_turned, 1)

            pe.wait_ge(wts_in, 16 * WEIGHTS)
            pe.wait_ge(bias_ready, 1)
            pe.wait_ge(digits_ready, 1)

            def pick_counts(b, s, j):
                if j == 0:
                    pe.wait_ge(picks_ready, at(b + 1))
                    need(pe, deg_picked, b - 1)
                for c in range(HCH):
                    for d in range(2):
                        last = pe.matmul(ps[s][:, j * P:(j + 1) * P], picks[:, s, c, j * P:(j + 1) * P],
                                         digits[:, d, c * P:(c + 1) * P], start=c + d == 0,
                                         stop=c == HCH - 1 and d == 1)
                if j == TB - 1:
                    last.then_inc(counts_picked, 1)

            def tile_sum(b, u, j):
                s = u % 2
                t = b * TB + j
                if j == 0:
                    pe.wait_ge(msg_ready, at(b + 1))
                    pe.wait_ge(masks_ready, at(b + 1))
                need(pe, scaled_ready, t - 1)
                first = isinstance(t, int) and t == 0
                last = pe.matmul(ps[6 + j % 2][:, 0:D], same[:, s, j, :], msg[:, s, j, :], start=True, stop=first)
                if not first:
                    pe.wait_ge(sums_ready, at(t))
                    last = pe.matmul(ps[6 + j % 2][:, 0:D], carry[:, s, j, :], sums[:, (j - 1) % 2, :],
                                     start=False, stop=True)
                last.then_inc(tile_summed, 1)

            def edge_step(b, u):
                s = u % 2
                if live(b, BATCHES):
                    loads = (b // 2 + 1) * 16 + (16 if isinstance(b, int) and b * W + W > E else 0)
                    pe.wait_ge(ea_in[s], at(loads))
                    need(pe, eaT_ready, b)
                    apart(pe, pe_passed)
                    for j in range(TB):
                        last = pe.transpose(ps[2][0:ED, j * P:(j + 1) * P], ea[:, s, j, :], ident[:, :])
                    last.then_inc(eaT_done, 1)
                if live(b - 1, BATCHES):
                    tile_sum(b - 1, u - 1, 0)
                if live(b + 1, BATCHES):
                    pick_counts(b + 1, 1 - s, 0)
                if live(b, BATCHES):
                    pe.wait_ge(eaT_ready, at(b + 1))
                    need(pe, h_ready, b)
                    pe.matmul(ps[3][:, :], w1e[:, :], eaT[:, s, :], start=True, stop=True).then_inc(h_done, 1)
                if live(b - 1, BATCHES):
                    tile_sum(b - 1, u - 1, 1)
                if live(b + 1, BATCHES):
                    pick_counts(b + 1, 1 - s, 1)
                if live(b, BATCHES):
                    need(pe, msg_ready, b - 1)
                    pe.matmul(ps[4 + s][:, :], ones_b[:, :], bias[:, 0, :, :].rearrange("p j d -> p (j d)"),
                              start=True, stop=False)
                    pe.wait_ge(h_ready, at(b + 1))
                    for j in range(TB):
                        last = pe.matmul(ps[4 + s][:, j * P:(j + 1) * P], he[:, s, j * P:(j + 1) * P], w2e[:, :],
                                         start=False, stop=j == TB - 1)
                    last.then_inc(m_done, 1)
                if live(b - 1, BATCHES):
                    tile_sum(b - 1, u - 1, 2)
                if live(b + 1, BATCHES):
                    pick_counts(b + 1, 1 - s, 2)
                if live(b - 1, BATCHES):
                    tile_sum(b - 1, u - 1, 3)
                if live(b + 1, BATCHES):
                    pick_counts(b + 1, 1 - s, 3)

            for j in range(TB):
                pick_counts(0, 0, j)
            run(pe, BATCHES, 2, edge_step, tail=1, peel=1)

            def node_step(n, u):
                m, s = n - 4, (u - 4) % 2
                if live(m, STEPS):
                    need(pe, res_ready, m - 1)
                    pe.matmul(ps[4 + s][:, :], ones_b[:, :], bias[:, 1, :, :].rearrange("p j d -> p (j d)"),
                              start=True, stop=False)
                    pe.wait_ge(hn_ready, at(m + 1))
                    for j in range(TB):
                        last = pe.matmul(ps[4 + s][:, j * P:(j + 1) * P], hn[:, s, j * P:(j + 1) * P], w2n[:, :],
                                         start=False, stop=j == TB - 1)
                    last.then_inc(o_done, 1)
                m, s = n - 1, (u - 1) % 2
                if live(m, STEPS):
                    pe.wait_ge(comb_ready, at(m + 1))
                    need(pe, cT_ready, m - 1)
                    for j in range(TB):
                        last = pe.transpose(ps[s][:, j * P:(j + 1) * P], comb[:, s, j, :], ident[:, :])
                    last.then_inc(cT_done, 1)
                m, s = n - 2, (u - 2) % 2
                if live(m, STEPS):
                    pe.wait_ge(cT_ready, at(m + 1))
                    need(pe, hn_ready, m - 1)
                    pe.matmul(ps[2 + s][:, :], w1n[:, :], cT[:, s, :], start=True, stop=True).then_inc(hn_done, 1)

            run(pe, STEPS, SPB * XR, node_step, tail=4)


_INS = ['x', 'src', 'dst', 'edge_attr_64', 'L0_gnn_W1n', 'L0_gnn_b1n', 'L0_gnn_W2n', 'L0_gnn_b2n', 'L0_gnn_W1e',
        'L0_gnn_b1e', 'L0_gnn_W2e', 'L0_gnn_b2e', 'L0_gnn_gin_eps', 'L0_gnn_rms_w']


def kernel(**inputs):
    import numpy as _np
    import concourse.bacc as _bacc
    from concourse import mybir as _mybir
    from concourse.bass_utils import run_bass_kernel_spmd as _run

    nc = _bacc.Bacc("TRN2", target_bir_lowering=False, num_devices=1)
    arrays, args = {}, []
    for name in _INS:
        a = _np.asarray(inputs[name])
        a = _np.ascontiguousarray(a.reshape(a.shape or (1,)))
        arrays[f"in_{name}"] = a
        args.append(nc.dram_tensor(f"in_{name}", a.shape, _mybir.dt.from_np(a.dtype), kind="ExternalInput").ap())
    out = nc.dram_tensor("out_0", arrays["in_x"].shape, _mybir.dt.float32, kind="ExternalOutput").ap()
    build(nc, *args, out)
    r = _run(nc, [arrays], core_ids=[0])
    return r.results[0]["out_0"]
```
